# Optimizing a Trainium2 kernel written in Bass

```python
import numpy as np
import jax
import jax.numpy as jnp

def _softmax(x, axis=-1):
    return jax.nn.softmax(x, axis=axis)

def _gelu(x):
    return jax.nn.gelu(x, approximate=True)

def _silu(x):
    return jax.nn.silu(x)

def _sigmoid(x):
    return jax.nn.sigmoid(x)

def _layernorm(x, axis=-1, eps=1e-05):
    m = jnp.mean(x, axis=axis, keepdims=True)
    v = jnp.var(x, axis=axis, keepdims=True)
    return (x - m) / jnp.sqrt(v + eps)

def _scatter_add(tgt, idx, src, axis=0):
    return tgt.at[idx].add(src)

def _segment_sum(src, seg, n):
    return jax.ops.segment_sum(src, seg, n)
kernel_name = 'mk_gnn_preln_d4_gnn_r8_d9ea29'

def setup_inputs(seed: int=0):
    np.random.seed(seed)
    _w = jnp.asarray

    def _rec_inputs():
        import jax
        import jax.numpy as jnp
        _gk = jax.random.key(seed)
        x = -0.0005121 + 1.001 * jax.random.normal(jax.random.fold_in(_gk, 1), (12500, 64), jnp.float32)
        src = jax.random.randint(jax.random.fold_in(_gk, 2), (200000,), 0, 12500, jnp.int32)
        dst = jax.random.randint(jax.random.fold_in(_gk, 3), (200000,), 0, 12500, jnp.int32)
        _o = jnp.argsort(dst, stable=True)
        src = src[_o]
        dst = dst[_o]
        edge_attr_8 = -4.12889e-05 + 1 * jax.random.normal(jax.random.fold_in(_gk, 12), (200000, 8), jnp.float32)
        return (x, src, dst, edge_attr_8)
    x, src, dst, edge_attr_8 = _rec_inputs()

    def _L0_gnn_setup():
        import jax, jax.numpy as jnp
        import numpy as np
        N_NODES = 6250
        N_EDGES = 100000
        D = 64
        N_BASIS = 8
        key = jax.random.key(seed)
        ks = jax.random.split(key, 16)
        inp = {'p': jax.random.normal(ks[0], (N_NODES, D), dtype=jnp.float32), 'idx_i': jax.random.randint(ks[1], (N_EDGES,), 0, N_NODES), 'idx_j': jax.random.randint(ks[2], (N_EDGES,), 0, N_NODES), 'basis': jax.random.normal(ks[3], (N_EDGES, N_BASIS), dtype=jnp.float32), 'pp_W1': jax.random.normal(ks[4], (D, D), dtype=jnp.float32) / np.sqrt(D), 'pp_b1': jnp.zeros((D,), dtype=jnp.float32), 'pp_W2': jax.random.normal(ks[5], (D, D), dtype=jnp.float32) / np.sqrt(D), 'pp_b2': jnp.zeros((D,), dtype=jnp.float32), 'pi_W1': jax.random.normal(ks[6], (2 * D, D), dtype=jnp.float32) / np.sqrt(2 * D), 'pi_b1': jnp.zeros((D,), dtype=jnp.float32), 'pi_W2': jax.random.normal(ks[7], (D, D), dtype=jnp.float32) / np.sqrt(D), 'pi_b2': jnp.zeros((D,), dtype=jnp.float32), 'pi_W3': jax.random.normal(ks[8], (D, D * N_BASIS), dtype=jnp.float32) / np.sqrt(D), 'ii_W1': jax.random.normal(ks[9], (D, D), dtype=jnp.float32) / np.sqrt(D), 'ii_b1': jnp.zeros((D,), dtype=jnp.float32), 'ii_W2': jax.random.normal(ks[10], (D, D), dtype=jnp.float32) / np.sqrt(D), 'ii_b2': jnp.zeros((D,), dtype=jnp.float32)}
        return inp
    _L0_gnn_all = _L0_gnn_setup()
    _L0_gnn_in = {k: v for k, v in _L0_gnn_all.items() if k in ('pp_W1', 'pp_b1', 'pp_W2', 'pp_b2', 'pi_W1', 'pi_b1', 'pi_W2', 'pi_b2', 'pi_W3', 'ii_W1', 'ii_b1', 'ii_W2', 'ii_b2')}
    del _L0_gnn_all

    def _L1_gnn_setup():
        import jax, jax.numpy as jnp
        import numpy as np
        N = 12500
        D = 64
        E = 125000

        def _gcn_layer(x, src, dst, W):
            n = x.shape[0]
            deg = jax.ops.segment_sum(jnp.ones_like(dst, dtype=x.dtype), dst, num_segments=n)
            deg_inv_sqrt = jax.lax.rsqrt(deg + 1.0)
            h = x * deg_inv_sqrt[:, None]
            agg = jax.ops.segment_sum(h[src], dst, num_segments=n)
            agg = (agg + x) * deg_inv_sqrt[:, None]
            return jax.nn.relu(agg @ W.T)
        key = jax.random.key(seed)
        k1, k2, k3, k4, k5 = jax.random.split(key, 5)
        x = jax.random.normal(k1, (N, D), dtype=jnp.float32)
        edge_index = jax.random.randint(k2, (2, E), 0, N, dtype=jnp.int64)

        def xavier(k, shape):
            limit = float(np.sqrt(6.0 / (shape[0] + shape[1])))
            return jax.random.uniform(k, shape, dtype=jnp.float32, minval=-limit, maxval=limit)
        W1 = xavier(k3, (D, D))
        W2 = xavier(k4, (D, D))
        W3 = xavier(k5, (D, D))
        return {'x': x, 'edge_index': edge_index, 'W1': W1, 'W2': W2, 'W3': W3}
    _L1_gnn_all = _L1_gnn_setup()
    _L1_gnn_in = {k: v for k, v in _L1_gnn_all.items() if k in ('W1', 'W2', 'W3')}
    del _L1_gnn_all

    def _L2_gnn_setup():
        import jax, jax.numpy as jnp
        import numpy as np
        NUM_NODES = 12500
        EMB_DIM = 64
        NUM_LAYERS = 3
        NUM_EDGES = 200000
        key = jax.random.key(seed)
        k_edge, k_emb = jax.random.split(key)
        edge_index = jax.random.randint(k_edge, (2, NUM_EDGES), 0, NUM_NODES, dtype=jnp.int32)
        emb = jax.random.normal(k_emb, (NUM_NODES, EMB_DIM), dtype=jnp.float32) * 0.01
        return {'edge_index': edge_index, 'emb': emb}
    _L2_gnn_all = _L2_gnn_setup()
    _L2_gnn_in = {k: v for k, v in _L2_gnn_all.items() if k in ()}
    del _L2_gnn_all

    def _L3_gnn_setup():
        import jax, jax.numpy as jnp
        import numpy as np
        N_NODES = 12500
        N_EDGES = 200000
        D_IN = 64
        D_OUT = 64
        key = jax.random.key(seed)
        k_x, k_e, k_w1, k_b1, k_w2, k_b2 = jax.random.split(key, 6)
        x = jax.random.normal(k_x, (N_NODES, D_IN), dtype=jnp.float32)
        edge_index = jax.random.randint(k_e, (2, N_EDGES), 0, N_NODES, dtype=jnp.int64)
        s1 = 1.0 / np.sqrt(D_IN)
        s2 = 1.0 / np.sqrt(D_OUT)
        W1 = jax.random.uniform(k_w1, (D_OUT, D_IN), minval=-s1, maxval=s1, dtype=jnp.float32)
        b1 = jax.random.uniform(k_b1, (D_OUT,), minval=-s1, maxval=s1, dtype=jnp.float32)
        W2 = jax.random.uniform(k_w2, (D_OUT, D_OUT), minval=-s2, maxval=s2, dtype=jnp.float32)
        b2 = jax.random.uniform(k_b2, (D_OUT,), minval=-s2, maxval=s2, dtype=jnp.float32)
        eps = jnp.float32(0.0)
        return {'x': x, 'edge_index': edge_index, 'eps': eps, 'W1': W1, 'b1': b1, 'W2': W2, 'b2': b2}
    _L3_gnn_all = _L3_gnn_setup()
    _L3_gnn_in = {k: v for k, v in _L3_gnn_all.items() if k in ('eps', 'W1', 'b1', 'W2', 'b2')}
    del _L3_gnn_all
    return {'x': x, 'src': src, 'dst': dst, 'edge_attr_8': edge_attr_8, 'L0_gnn_pp_W1': _L0_gnn_in['pp_W1'], 'L0_gnn_pp_b1': _L0_gnn_in['pp_b1'], 'L0_gnn_pp_W2': _L0_gnn_in['pp_W2'], 'L0_gnn_pp_b2': _L0_gnn_in['pp_b2'], 'L0_gnn_pi_W1': _L0_gnn_in['pi_W1'], 'L0_gnn_pi_b1': _L0_gnn_in['pi_b1'], 'L0_gnn_pi_W2': _L0_gnn_in['pi_W2'], 'L0_gnn_pi_b2': _L0_gnn_in['pi_b2'], 'L0_gnn_pi_W3': _L0_gnn_in['pi_W3'], 'L0_gnn_ii_W1': _L0_gnn_in['ii_W1'], 'L0_gnn_ii_b1': _L0_gnn_in['ii_b1'], 'L0_gnn_ii_W2': _L0_gnn_in['ii_W2'], 'L0_gnn_ii_b2': _L0_gnn_in['ii_b2'], 'L1_gnn_W1': _L1_gnn_in['W1'], 'L1_gnn_W2': _L1_gnn_in['W2'], 'L1_gnn_W3': _L1_gnn_in['W3'], 'L3_gnn_eps': _L3_gnn_in['eps'], 'L3_gnn_W1': _L3_gnn_in['W1'], 'L3_gnn_b1': _L3_gnn_in['b1'], 'L3_gnn_W2': _L3_gnn_in['W2'], 'L3_gnn_b2': _L3_gnn_in['b2']}

def reference(x, src, dst, edge_attr_8, L0_gnn_pp_W1, L0_gnn_pp_b1, L0_gnn_pp_W2, L0_gnn_pp_b2, L0_gnn_pi_W1, L0_gnn_pi_b1, L0_gnn_pi_W2, L0_gnn_pi_b2, L0_gnn_pi_W3, L0_gnn_ii_W1, L0_gnn_ii_b1, L0_gnn_ii_W2, L0_gnn_ii_b2, L1_gnn_W1, L1_gnn_W2, L1_gnn_W3, L3_gnn_eps, L3_gnn_W1, L3_gnn_b1, L3_gnn_W2, L3_gnn_b2):
    import jax
    import jax.numpy as jnp

    def _L0_gnn_ref(p, idx_i, idx_j, basis, pp_W1, pp_b1, pp_W2, pp_b2, pi_W1, pi_b1, pi_W2, pi_b2, pi_W3, ii_W1, ii_b1, ii_W2, ii_b2):
        import jax, jax.numpy as jnp
        import numpy as np
        N_NODES = 6250
        N_EDGES = 100000
        D = 64
        N_BASIS = 8
        p1 = jnp.tanh(p @ pp_W1 + pp_b1) @ pp_W2 + pp_b2
        inter = jnp.concatenate([p1[idx_i], p1[idx_j]], axis=-1)
        inter = inter @ pi_W1 + pi_b1
        inter = inter @ pi_W2 + pi_b2
        inter = inter @ pi_W3
        inter = inter.reshape(inter.shape[0], D, N_BASIS)
        i1 = jnp.einsum('ecb,eb->ec', inter, basis)
        i1 = jnp.tanh(i1 @ ii_W1 + ii_b1) @ ii_W2 + ii_b2
        out = jax.ops.segment_sum(i1, idx_j, num_segments=p1.shape[0])
        return out

    def _L1_gnn_ref(x, edge_index, W1, W2, W3):
        import jax, jax.numpy as jnp
        import numpy as np
        N = 12500
        D = 64
        E = 125000

        def _gcn_layer(x, src, dst, W):
            n = x.shape[0]
            deg = jax.ops.segment_sum(jnp.ones_like(dst, dtype=x.dtype), dst, num_segments=n)
            deg_inv_sqrt = jax.lax.rsqrt(deg + 1.0)
            h = x * deg_inv_sqrt[:, None]
            agg = jax.ops.segment_sum(h[src], dst, num_segments=n)
            agg = (agg + x) * deg_inv_sqrt[:, None]
            return jax.nn.relu(agg @ W.T)
        src, dst = (edge_index[0], edge_index[1])
        h = _gcn_layer(x, src, dst, W1)
        h = _gcn_layer(h, src, dst, W2)
        h = _gcn_layer(h, src, dst, W3)
        return h

    def _L2_gnn_ref(edge_index, emb):
        import jax, jax.numpy as jnp
        import numpy as np
        NUM_NODES = 12500
        EMB_DIM = 64
        NUM_LAYERS = 3
        NUM_EDGES = 200000
        src, dst = (edge_index[0], edge_index[1])
        n = emb.shape[0]
        deg = jax.ops.segment_sum(jnp.ones_like(src, dtype=emb.dtype), dst, num_segments=n)
        dinv = jnp.where(deg > 0, jax.lax.rsqrt(jnp.maximum(deg, 1.0)), 0.0)
        norm = dinv[src] * dinv[dst]
        x = emb
        out = emb
        for _ in range(NUM_LAYERS):
            msgs = norm[:, None] * x[src]
            x = jax.ops.segment_sum(msgs, dst, num_segments=n)
            out = out + x
        return out / (NUM_LAYERS + 1)

    def _L3_gnn_ref(x, edge_index, eps, W1, b1, W2, b2):
        import jax, jax.numpy as jnp
        import numpy as np
        N_NODES = 12500
        N_EDGES = 200000
        D_IN = 64
        D_OUT = 64
        src = edge_index[0]
        dst = edge_index[1]
        agg = jax.ops.segment_sum(x[src], dst, num_segments=x.shape[0])
        h = (1.0 + eps) * x + agg
        h = jax.nn.relu(h @ W1.T + b1)
        h = h @ W2.T + b2
        return h
    edge_index = jnp.stack([src, dst])
    h = jnp.maximum(_layernorm(x, axis=-1), 0.0)
    x = x + _L0_gnn_ref(h, src, dst, edge_attr_8, L0_gnn_pp_W1, L0_gnn_pp_b1, L0_gnn_pp_W2, L0_gnn_pp_b2, L0_gnn_pi_W1, L0_gnn_pi_b1, L0_gnn_pi_W2, L0_gnn_pi_b2, L0_gnn_pi_W3, L0_gnn_ii_W1, L0_gnn_ii_b1, L0_gnn_ii_W2, L0_gnn_ii_b2)
    h = jnp.maximum(_layernorm(x, axis=-1), 0.0)
    x = x + _L1_gnn_ref(h, edge_index, L1_gnn_W1, L1_gnn_W2, L1_gnn_W3)
    h = jnp.maximum(_layernorm(x, axis=-1), 0.0)
    x = x + _L2_gnn_ref(edge_index, h)
    h = jnp.maximum(_layernorm(x, axis=-1), 0.0)
    x = x + _L3_gnn_ref(h, edge_index, L3_gnn_eps, L3_gnn_W1, L3_gnn_b1, L3_gnn_W2, L3_gnn_b2)
    return x

_drawn_inputs = setup_inputs


def setup_inputs(seed=0):
    import zlib

    import numpy as np

    out = dict(_drawn_inputs(seed))
    spreads = {'L0_gnn_pp_b1': (0.0, 0.1),
     'L0_gnn_pp_b2': (0.0, 0.1),
     'L0_gnn_pi_b1': (0.0, 0.1),
     'L0_gnn_pi_b2': (0.0, 0.1),
     'L0_gnn_ii_b1': (0.0, 0.1),
     'L0_gnn_ii_b2': (0.0, 0.1)}
    factors = {'L3_gnn_b1': 8.0, 'L3_gnn_b2': 3.185}
    for name, (base, spread) in spreads.items():
        noise = np.random.default_rng([zlib.crc32(name.encode()), seed]).standard_normal(out[name].shape)
        drawn = base * np.exp(spread * noise) if base else spread * noise
        out[name] = jnp.asarray(drawn.astype(out[name].dtype))
    for name, factor in factors.items():
        out[name] = (out[name] * factor).astype(out[name].dtype)
    return out
```

```python
import numpy as np
import concourse.bass as bass
from concourse import mybir
from contextlib import ExitStack

F32 = mybir.dt.float32
F16 = mybir.dt.float16
F8 = mybir.dt.float8e4
I32 = mybir.dt.int32
U8 = mybir.dt.uint8
ALU = mybir.AluOpType
ACT = mybir.ActivationFunctionType
AX = mybir.AxisListType

P = 128
D = 64
NB = 8
N_NODES = 12500
N_EDGES = 200000
TILES = -(-N_NODES // P)
NP = TILES * P
TAIL = N_NODES - (TILES - 1) * P
GROUPS = 7
GT = TILES // GROUPS
GC = GT * P
BANKS = 4
BC = GC // BANKS
LO = 2048.0

A_BYTES = GROUPS * NP * GC
KC = 2
CHUNKS = TILES // KC
SLOTS = 7

W = P
ET = 8
EG = ET * P
STEPS = 98
EGROUPS = 2 * STEPS
ETILES = EGROUPS * ET
EP = ETILES * P

SPAN = -(-N_EDGES // P)
SHIFTS = 7 * GROUPS
KW = SPAN + 2 * SHIFTS
SC = 16
PLAN = 2 * ET + ET // 4
assert SPAN <= EGROUPS * ET and EGROUPS * ET - SPAN < ET

LAYERS = 7


class Chain:

    def __init__(self, eng, sem, start=0):
        self.eng, self.sem, self.start, self.n = eng, sem, start, 0

    def mark(self, ins):
        ins.then_inc(self.sem, 1)
        self.n += 1

    def wait(self):
        self.eng.wait_ge(self.sem, self.start + self.n)

    def __call__(self, ins):
        self.mark(ins)
        self.wait()


def centre_and_scale(nc, ch, x, xc, sq, small, out, var_ready, root_ready, n):
    wide = [P, GT, D]
    s1, mean, s2, rstd = (small[:, i, :] for i in range(4))
    ch(nc.vector.tensor_reduce(out=s1, in_=x, op=ALU.add, axis=AX.X))
    ch(nc.vector.tensor_scalar(mean, s1, -1.0 / D, None, ALU.mult))
    ch(nc.vector.tensor_tensor(xc, x, mean.unsqueeze(2).to_broadcast(wide), ALU.add))
    ch(nc.vector.scalar_tensor_tensor(out=sq, in0=xc, scalar=1.0 / D, in1=xc, op0=ALU.mult, op1=ALU.mult))
    nc.vector.tensor_reduce(out=s2, in_=sq, op=ALU.add, axis=AX.X).then_inc(var_ready, 1)
    ch.eng.wait_ge(root_ready, n)
    ch(nc.vector.reciprocal(rstd, s2))
    return nc.vector.scalar_tensor_tensor(out=out, in0=xc, scalar=0.0,
                                          in1=rstd.unsqueeze(2).to_broadcast(wide), op0=ALU.max, op1=ALU.mult)


def split(nc, ch, v, table, tmp):
    ch(nc.vector.tensor_copy(table[:, :, 0:D], v))
    ch(nc.vector.tensor_tensor(tmp, v, table[:, :, 0:D], ALU.subtract))
    return nc.vector.tensor_scalar(table[:, :, D:2 * D], tmp, LO, None, ALU.mult)


def build(nc, w, out, debug=None):
    x, srcT, dstT, src_row, dst_row, basisT = (w[n] for n in ("x", "srcT", "dstT", "src_row", "dst_row", "basisT"))
    A = nc.dram_tensor("counts", (A_BYTES,), U8, kind="Internal").ap()
    Us = nc.dram_tensor("u_source", (NP, 2 * D), F32, kind="Internal").ap()
    Ud = nc.dram_tensor("u_target", (NP + W, 2 * D), F32, kind="Internal").ap()
    A_cells = A.rearrange("(n a) -> n a", a=1)
    A_blocks = A.rearrange("(g p k c) -> g p k c", g=GROUPS, p=P, k=TILES)
    A_flat = A.rearrange("(p n) -> p n", p=P)

    with ExitStack() as ctx:
        sb = lambda n, s, d: ctx.enter_context(nc.sbuf_tensor(n, s, d))
        sem = lambda n: ctx.enter_context(nc.semaphore(n))
        T = {}
        T["x"] = sb("x_sb", [P, TILES, D], F32)
        T["ident"] = sb("ident", [P, P], F32)
        T["M"] = sb("M_sb", [P, 4, D], F32)
        T["c2"] = sb("c2", [P, 1], F32)
        T["iib1"] = sb("iib1", [P, D], F32)
        T["ones"] = sb("ones", [1, P], F32)
        T["nodeid"] = sb("nodeid", [P, EGROUPS + 1], F32)
        T["eps"] = sb("eps", [P, 1], F32)
        T["deg"] = sb("deg", [P, TILES], F32)
        T["iota_w"] = sb("iota_w", [P, W], F32)
        with ExitStack() as edge:
            esb = lambda n, s, d: edge.enter_context(nc.sbuf_tensor(n, s, d))
            T["plan"] = esb("plan", [P, EGROUPS + 1, PLAN], I32)
            T["dloc"] = esb("dloc", [P, ETILES + ET], F32)
            zero = esb("zero", [P, 12544], U8)
            zeroed = [sem("zeroed0"), sem("zeroed1")]
            T["zeroed"] = zeroed
            prepare(nc, ctx, T, A_flat, zero, zeroed, x, srcT, dstT, src_row, dst_row, w, Us, Ud)
            T["aggT"] = esb("aggT", [D + 1, NP + W], F32)
            T["zero"] = zero
            edges(nc, ctx, T, A_cells, Us, Ud, w)
            after_edges(nc, T, w)
        dense(nc, T, A_blocks, w, out)


def prepare(nc, ctx, T, A_flat, zero, zeroed, x, srcT, dstT, src_row, dst_row, w, Us, Ud):
    with ExitStack() as c:
        sb = lambda n, s, d: c.enter_context(nc.sbuf_tensor(n, s, d))
        ps = lambda n, s: c.enter_context(nc.psum_tensor(n, s, F32))
        sem = lambda n: c.enter_context(nc.semaphore(n))
        x_sb, ident = T["x"], T["ident"]
        sA, dA = sb("sA", [P, KW], I32), sb("dA", [P, KW], I32)
        key = sb("key", [P, KW], I32)
        t1, t2, gidx = sb("t1", [P, KW], I32), sb("t2", [P, KW], I32), sb("gidx", [P, KW], I32)
        later, earlier = sb("later", [P, SPAN], F32), sb("earlier", [P, SPAN], F32)
        dT = sb("dT", [P, ETILES], I32)
        count = sb("count", [P, SPAN + 1], F8)
        base_row = sb("base_row", [1, EGROUPS], F32)
        base_bc = sb("base_bc", [P, EGROUPS], F32)
        iota_i = sb("iota_i", [P, W + 1], I32)
        iota_p = sb("iota_p", [P, 1], F32)
        xc, sq, hst = (sb(n, [P, GT, D], F32) for n in ("xc0", "sq0", "hst0"))
        small = sb("small0", [P, 4, GT], F32)
        hT, t1T, p1T = (sb(n, [D, GC], F32) for n in ("hT0", "t1T", "p1T"))
        us, ud = sb("us", [P, GT, 2, D], F32), sb("ud", [P, GT, 2, D], F32)
        ppW1, ppW2, piW2, iiW1 = (sb(n, [D, D], F32) for n in ("ppW1", "ppW2", "piW2", "iiW1"))
        piW1T = sb("piW1T", [D, 2 * D], F32)
        piW2d = sb("piW2d", [D, 2, D], F32)
        W3T = sb("W3T", [D, NB, D], F32)
        ppb1, ppb2, pib1 = (sb(n, [D, 1], F32) for n in ("ppb1", "ppb2", "pib1"))
        pib2 = sb("pib2", [P, 1], F32)
        Cab = sb("Cab", [D, 2 * D], F32)
        psA = ps("psA", [P, 4, 512])
        psB = ps("psB", [P, 4, 512])

        S = {n: sem("p_" + n) for n in (
            "x keys plan0 srcT dT w iotas id0 ident dve wts wtsdone base basebc h_ready tp tp_ev z1 z1_ev z2 z2_ev tb tb_ev st zinit var root eps passed".split())}
        n_weights = 12
        blk = c.enter_context(nc.Block())

        @blk.sync
        def _(sp):
            sp.dma_start(x_sb[:, 0:TILES - 1, :], x[0:(TILES - 1) * P, :].rearrange("(k p) d -> p k d", p=P)).then_inc(S["x"], 16)
            sp.wait_ge(S["zinit"], 2)
            sp.dma_start(x_sb[0:TAIL, TILES - 1, :], x[(TILES - 1) * P:N_NODES, :]).then_inc(S["x"], 16)
            for r, t in ((src_row, sA), (dst_row, dA)):
                lap = bass.AP(tensor=r.tensor, offset=r.offset, ap=[[SPAN, P], [1, KW]])
                sp.dma_start(t[:, :], lap).then_inc(S["keys"], 16)
            sp.wait_ge(S["plan0"], 1)
            sp.dma_start(T["plan"][:, 0:EGROUPS, 0:ET], srcT.rearrange("p (g t) -> p g t", t=ET)).then_inc(S["srcT"], 16)
            sp.dma_start(dT[:, :], dstT).then_inc(S["dT"], 16)
            with sp.Fori(0, GROUPS) as g:
                sp.wait_ge(S["tb_ev"], 4 * g + 4)
                sp.dma_start(Us.rearrange("(k p) d -> p k d", p=P)[:, bass.ds(g * GT, GT), :], us[:, :, :, :].rearrange("p k h d -> p k (h d)")).then_inc(S["st"], 16)
                sp.dma_start(Ud[0:NP, :].rearrange("(k p) d -> p k d", p=P)[:, bass.ds(g * GT, GT), :], ud[:, :, :, :].rearrange("p k h d -> p k (h d)")).then_inc(S["st"], 16)
            sp.dma_start(Ud[NP:NP + W, :], x_sb[:, 0:2, :].rearrange("p k d -> p (k d)")).then_inc(S["st"], 16)
            sp.wait_ge(S["st"], 16 * (2 * GROUPS + 1))
            sp.wait_ge(S["srcT"], 16)

        @blk.gpsimd
        def _(pool):
            nc.gpsimd.memset(zero[:, :], 0).then_inc(S["zinit"], 1)
            nc.gpsimd.memset(x_sb[:, TILES - 1, :], 0.0).then_inc(S["zinit"], 1)
            nc.gpsimd.memset(ident[:, :], 0.0).then_inc(S["id0"], 1)
            pool.wait_ge(S["id0"], 1)
            pool.affine_select(out=ident[:, :], in_=ident[:, :], compare_op=ALU.not_equal, fill=1.0,
                               base=0, pattern=[[-1, P]], channel_multiplier=1).then_inc(S["ident"], 1)
            nc.gpsimd.iota(iota_i[:, 0:W], pattern=[[1, W]], base=0, channel_multiplier=0).then_inc(S["iotas"], 1)
            nc.gpsimd.iota(iota_i[:, W:W + 1], pattern=[[0, 1]], base=0, channel_multiplier=1).then_inc(S["iotas"], 1)
            pool.wait_ge(S["zinit"], 2)
            pool.wait_ge(S["x"], 32)
            pool.wait_ge(S["keys"], 32)
            pool.wait_ge(S["dT"], 16)
            width = zero.shape[1]
            def fill(i, q):
                pool.dma_start(A_flat[:, bass.ds((2 * i + q) * width, width)], zero[:, :]).then_inc(zeroed[q], 16)

            fill(0, 0)
            fill(0, 1)
            with pool.Fori(0, A_BYTES // P // width // 2 - 1) as i:
                for q in range(2):
                    pool.wait_ge(zeroed[q], 16 * i + 16)
                    pool.sem_inc(S["passed"], 1)
                    fill(i + 1, q)

        @blk.scalar
        def _(act):
            loads = [(ppW1[:, :], w["pp_W1"]), (ppW2[:, :], w["pp_W2"]), (piW2[:, :], w["pi_W2"]), (iiW1[:, :], w["ii_W1"]),
                     (piW1T[:, :], w["pi_W1T"]), (W3T[:, :, :], w["pi_W3T"]),
                     (ppb1[:, :], w["pp_b1"]), (ppb2[:, :], w["pp_b2"]), (pib1[:, :], w["pi_b1"]),
                     (pib2[0:D, :], w["pi_b2"]), (pib2[D:P, :], w["pi_b2"]), (T["iib1"][:, :], w["ii_b1"].to_broadcast([P, D]))]
            assert len(loads) == n_weights
            for t, a in loads:
                act.dma_start(t, a).then_inc(S["w"], 16)
            act.wait_ge(S["w"], 16 * n_weights)
            act.wait_ge(S["dve"], 1)
            act.wait_ge(S["wts"], 1)
            nc.scalar.copy(Cab[:, :], psA[0:D, 0, 0:2 * D])
            nc.scalar.activation(T["c2"][:, :], psA[:, 1, 0:1], ACT.Identity, bias=pib2[:, :])
            nc.scalar.copy(T["M"][:, :, :], psA[:, 2, 0:4 * D].rearrange("p (c m) -> p c m", c=4)).then_inc(S["wtsdone"], 1)
            cols = [512, 512, 512, GC - 3 * 512]
            act.wait_ge(S["eps"], 1)
            with act.Fori(0, GROUPS) as g:
                act.wait_ge(S["var"], g + 1)
                nc.scalar.activation(small[:, 2, :], small[:, 2, :], ACT.Sqrt, bias=T["eps"][:, :]).then_inc(S["root"], 1)
                for b in range(4):
                    act.wait_ge(S["tp"], 4 * g + b + 1)
                    nc.scalar.copy(hT[:, 512 * b:512 * b + cols[b]], psA[0:D, b, 0:cols[b]]).then_inc(S["tp_ev"], 1)
                for b in range(4):
                    act.wait_ge(S["z1"], 4 * g + b + 1)
                    nc.scalar.activation(t1T[:, BC * b:BC * b + BC], psB[0:D, b, 0:BC], ACT.Tanh, bias=ppb1[:, :]).then_inc(S["z1_ev"], 1)
                for b in range(4):
                    act.wait_ge(S["z2"], 4 * g + b + 1)
                    nc.scalar.activation(p1T[:, BC * b:BC * b + BC], psA[0:D, b, 0:BC], ACT.Identity, bias=ppb2[:, :]).then_inc(S["z2_ev"], 1)
                act.wait_ge(S["st"], 32 * g)
                for b in range(4):
                    act.wait_ge(S["tb"], 4 * g + b + 1)
                    n = cols[b] // P
                    v = psB[:, b, 0:cols[b]].rearrange("p (k h d) -> p k h d", h=2, d=D)
                    twice = [P, n, 2, D]
                    nc.scalar.copy(us[:, 4 * b:4 * b + n, :, :], v[:, :, 0, :].unsqueeze(2).to_broadcast(twice))
                    nc.scalar.copy(ud[:, 4 * b:4 * b + n, :, :], v[:, :, 1, :].unsqueeze(2).to_broadcast(twice)).then_inc(S["tb_ev"], 1)

        @blk.vector
        def _(dve):
            ch = Chain(dve, S["dve"])
            nc.vector.memset(T["ones"][:, :], 1.0)
            nc.vector.memset(T["eps"][:, :], 1e-5).then_inc(S["eps"], 1)
            nc.vector.memset(T["nodeid"][:, EGROUPS:EGROUPS + 1], -1.0)
            nc.vector.memset(T["dloc"][:, ETILES:ETILES + ET], -1.0)
            nc.vector.memset(T["plan"][:, :, :], 0).then_inc(S["plan0"], 1)
            nc.vector.memset(later[:, :], 0.0)
            nc.vector.memset(earlier[:, :], 0.0)
            dve.wait_ge(S["plan0"], 1)
            nc.vector.memset(T["plan"][:, EGROUPS - 1:EGROUPS + 1, ET:2 * ET], 1 << 29)
            dve.wait_ge(S["w"], 16 * n_weights)
            ch(nc.vector.tensor_copy(piW2d[:, :, :], piW2[:, :].unsqueeze(1).to_broadcast([D, 2, D])))
            dve.wait_ge(S["keys"], 32)
            ch(nc.vector.tensor_scalar(gidx[:, :], dA[:, :], GC, None, ALU.is_ge))
            for i in range(2, GROUPS):
                ch(nc.vector.scalar_tensor_tensor(out=gidx[:, :], in0=dA[:, :], scalar=float(GC * i), in1=gidx[:, :], op0=ALU.is_ge, op1=ALU.add))
            nc.vector.tensor_scalar(t1[:, :], sA[:, :], 127, None, ALU.bitwise_and)
            ch(nc.vector.tensor_scalar(t2[:, :], sA[:, :], 7, None, ALU.logical_shift_right))
            ch(nc.vector.scalar_tensor_tensor(out=t1[:, :], in0=t1[:, :], scalar=float(TILES), in1=t2[:, :], op0=ALU.mult, op1=ALU.add))
            ch(nc.vector.tensor_scalar(t2[:, :], dA[:, :], 7, None, ALU.logical_shift_right))
            ch(nc.vector.scalar_tensor_tensor(out=t1[:, :], in0=t1[:, :], scalar=float(GT), in1=t2[:, :], op0=ALU.mult, op1=ALU.add))
            ch(nc.vector.scalar_tensor_tensor(out=t1[:, :], in0=gidx[:, :], scalar=float((NP - 1) * GT), in1=t1[:, :], op0=ALU.mult, op1=ALU.add))
            nc.vector.tensor_scalar(t2[:, :], dA[:, :], 127, None, ALU.bitwise_and)
            ch(nc.vector.tensor_scalar(t1[:, :], t1[:, :], 7, None, ALU.logical_shift_left))
            ch(nc.vector.tensor_tensor(key[:, :], t1[:, :], t2[:, :], ALU.bitwise_or))
            dve.wait_ge(S["dT"], 16)
            dve.wait_ge(S["iotas"], 2)
            nc.vector.tensor_copy(base_row[:, :], dT[0:1, :].rearrange("p (g t) -> p g t", t=ET)[:, :, 0]).then_inc(S["base"], 1)
            nc.vector.tensor_copy(T["iota_w"][:, :], iota_i[:, 0:W])
            ch(nc.vector.tensor_copy(iota_p[:, :], iota_i[:, W:W + 1]))
            dve.wait_ge(S["basebc"], 1)
            ch(nc.vector.tensor_copy(base_bc[:, :], psB[:, 0, 0:EGROUPS]))
            nc.vector.tensor_scalar(T["nodeid"][:, 0:EGROUPS], base_bc[:, :], iota_p[:, :], None, ALU.add)
            ch(nc.vector.tensor_tensor(T["dloc"][:, 0:ETILES].rearrange("p (g t) -> p g t", t=ET), dT[:, :].rearrange("p (g t) -> p g t", t=ET),
                                       base_bc[:, :].unsqueeze(2).to_broadcast([P, EGROUPS, ET]), ALU.subtract))
            dve.wait_ge(S["x"], 32)
            dve.wait_ge(S["zinit"], 2)
            before = ch.n
            step = 5 + 3 * (SHIFTS // GROUPS)
            reach = SPAN + SHIFTS
            diffs = (t1, t2)
            with dve.Fori(0, GROUPS) as g:
                ch = Chain(dve, S["dve"], before + g * step)
                dve.wait_ge(S["tp"], 4 * g)
                centre_and_scale(nc, ch, x_sb[:, bass.ds(g * GT, GT), :], xc[:, :, :], sq[:, :, :], small, hst[:, :, :],
                                 S["var"], S["root"], g + 1).then_inc(S["h_ready"], 1)
                for u in range(SHIFTS // GROUPS):
                    s = g * (SHIFTS // GROUPS) + (u + 1)
                    diff = diffs[u % 2]
                    ch(nc.vector.tensor_tensor(diff[:, 0:reach], key[:, 0:reach], key[:, bass.ds(s, reach)], ALU.bitwise_xor))
                    ch.mark(nc.vector.scalar_tensor_tensor(out=later[:, :], in0=diff[:, SHIFTS:reach], scalar=0.0, in1=later[:, :], op0=ALU.is_equal, op1=ALU.add))
                    ch.mark(nc.vector.scalar_tensor_tensor(out=earlier[:, :], in0=diff[:, bass.ds(SHIFTS - s, SPAN)], scalar=0.0, in1=earlier[:, :], op0=ALU.is_equal, op1=ALU.add))
                ch.wait()
                assert ch.n == step, ch.n
            ch = Chain(dve, S["dve"], before + GROUPS * step)
            full = SPAN // ET
            nc.vector.tensor_scalar(count[:, 0:SPAN], later[:, :], 1.0, None, ALU.add, saturate=False)
            ch(nc.vector.tensor_scalar(t2[:, 0:SPAN], earlier[:, :], 0.0, float(1 << 29), ALU.is_gt, ALU.mult))
            for groups, at, n in ((slice(0, full), slice(0, full * ET), ET), (slice(full, full + 1), slice(full * ET, SPAN), SPAN - full * ET)):
                cut = lambda a: a[:, at].rearrange("p (g t) -> p g t", t=n)
                keys = key[:, SHIFTS + at.start:SHIFTS + at.stop].rearrange("p (g t) -> p g t", t=n)
                nc.vector.tensor_tensor(T["plan"][:, groups, ET:ET + n], keys, cut(t2), ALU.bitwise_or)
                counts = T["plan"][:, groups, 2 * ET:PLAN].bitcast(U8)[:, :, 0:n]
                ch(nc.vector.tensor_copy(counts, cut(count).bitcast(U8)))

        @blk.tensor
        def _(pe):
            pe.wait_ge(S["dve"], 1)
            pe.wait_ge(S["w"], 16 * n_weights)
            mm = nc.tensor.matmul
            mm(psA[0:D, 0, 0:D], piW1T[:, 0:D], piW2[:, :], start=True, stop=True)
            mm(psA[0:D, 0, D:2 * D], piW1T[:, D:2 * D], piW2[:, :], start=True, stop=True)
            mm(psA[:, 1, 0:1], piW2d[:, :, :], pib1[:, :], start=True, stop=True)
            for q in range(4):
                last = mm(psA[:, 2, q * D:(q + 1) * D], W3T[:, 2 * q:2 * q + 2, :], iiW1[:, :], start=True, stop=True)
            last.then_inc(S["wts"], 1)
            pe.wait_ge(S["base"], 1)
            mm(psB[:, 0, 0:EGROUPS], T["ones"][:, :], base_row[:, :], start=True, stop=True).then_inc(S["basebc"], 1)
            pe.wait_ge(S["ident"], 1)
            pe.wait_ge(S["wtsdone"], 1)
            with pe.Fori(0, GROUPS) as g:
                pe.wait_ge(S["h_ready"], g + 1)
                pe.wait_ge(S["z2_ev"], 4 * g)
                pe.sem_inc(S["passed"], 1)
                for t in range(GT):
                    last = nc.tensor.transpose(psA[0:D, t // 4, (t % 4) * P:(t % 4 + 1) * P], hst[:, t, :], ident[:, :])
                    if t % 4 == 3 or t == GT - 1:
                        last.then_inc(S["tp"], 1)
                pe.wait_ge(S["tb_ev"], 4 * g)
                for b in range(4):
                    pe.wait_ge(S["tp_ev"], 4 * g + min(b + 1, 4))
                    pe.sem_inc(S["passed"], 1)
                    mm(psB[0:D, b, 0:BC], ppW1[:, :], hT[:, BC * b:BC * b + BC], start=True, stop=True).then_inc(S["z1"], 1)
                for b in range(4):
                    pe.wait_ge(S["z1_ev"], 4 * g + b + 1)
                    pe.sem_inc(S["passed"], 1)
                    mm(psA[0:D, b, 0:BC], ppW2[:, :], t1T[:, BC * b:BC * b + BC], start=True, stop=True).then_inc(S["z2"], 1)
                for t in range(GT):
                    if t % 4 == 0:
                        pe.wait_ge(S["z2_ev"], 4 * g + min(t // 4 + 2, 4))
                        pe.sem_inc(S["passed"], 1)
                    last = mm(psB[:, t // 4, (t % 4) * P:(t % 4 + 1) * P], p1T[:, t * P:(t + 1) * P], Cab[:, :], start=True, stop=True)
                    if t % 4 == 3 or t == GT - 1:
                        last.then_inc(S["tb"], 1)


def edges(nc, ctx, T, A_cells, Us, Ud, w):
    dst_seq, basisT = w["dst_seq"], w["basisT"]
    with ExitStack() as c:
        sb = lambda n, s, d: c.enter_context(nc.sbuf_tensor(n, s, d))
        ps = lambda n, s: c.enter_context(nc.psum_tensor(n, s, F32))
        sem = lambda n: c.enter_context(nc.semaphore(n))
        two = lambda f, n, *a: [f(f"{n}{q}", *a) for q in range(2)]
        basis = two(sb, "basis", [P, 4, EG], F32)
        dst_all = two(sb, "dst_all", [P, EG], I32)
        window = two(sb, "window", [P, 2 * D], F32)
        from_node = two(sb, "from_node", [P, EG], F32)
        to_node = two(sb, "to_node", [P, ET, W], F32)
        gathered = two(sb, "gathered", [P, ET, 2 * D], F32)
        u = two(sb, "u", [P, 512], F32)
        z = two(sb, "z", [P, 4, 512], F32)
        msg = two(sb, "msg", [P, ET, D + 1], F32)
        plan = two(sb, "plan_now", [P, PLAN], I32)
        ps_u = two(ps, "ps_u", [P, 512])
        ps_m = two(ps, "ps_m", [P, ET, D])
        ps_w = ps("ps_w", [P, W])
        aggT = T["aggT"]
        S = {n: sem("e_" + n) for n in "init staged0 staged1 from0 from1 to0 to1 loaded0 loaded1 rows0 rows1 cells0 cells1 u0 u1 u_out z_done m_done m_bias0 m_bias1 tanh0 tanh1 summed added passed".split()}
        blk = c.enter_context(nc.Block())
        base_of = lambda eng, g: eng.value_load(dst_seq[bass.ds((g + 1) * EG, 1)].unsqueeze(0), min_val=0, max_val=NP - 1)

        @blk.sync
        def _(sp):
            def load(t, q):
                g = 2 * t + q
                base = base_of(sp, g)
                sp.wait_ge(S["z_done"], 4 * t + 2 * q)
                for h in range(2):
                    rows = basisT[h:NB:2, bass.ds(g * EG, EG)]
                    rows = bass.AP(tensor=rows.tensor, offset=rows.offset, ap=[[0, D]] + [list(a) for a in rows.ap])
                    sp.dma_start(basis[q][h * D:(h + 1) * D, :, :], rows).then_inc(S[f"loaded{q}"], 16)
                sp.dma_start(dst_all[q][:, :], dst_seq[bass.ds((g + 1) * EG, EG)].unsqueeze(0).to_broadcast([P, EG])).then_inc(S[f"loaded{q}"], 16)
                sp.dma_start(window[q][:, :], Ud[bass.ds(base, W), :]).then_inc(S[f"loaded{q}"], 16)

            with sp.Fori(0, STEPS) as t:
                for q in range(2):
                    load(t, q)
            load(STEPS, 0)
            sp.wait_ge(S["loaded0"], 64 * (STEPS + 1))

        @blk.gpsimd
        def _(pool):
            for z0 in T["zeroed"]:
                pool.wait_ge(z0, 16 * (A_BYTES // P // T["zero"].shape[1] // 2))

            def gather(t, q):
                pool.wait_ge(S[f"u{q}"], 2 * t)
                pool.wait_ge(S[f"staged{q}"], t + 1)
                pool.sem_inc(S["passed"], 1)
                for i in range(ET):
                    pool.indirect_dma_start(gathered[q][:, i, :], None, Us, bass.IndirectOffsetOnAxis(ap=plan[q][:, i:i + 1], axis=0)).then_inc(S[f"rows{q}"], 16)

            def stage(t, q):
                pool.wait_ge(S[f"rows{q}"], 16 * ET * t)
                pool.wait_ge(S[f"cells{q}"], 16 * ET * t)
                pool.sem_inc(S["passed"], 1)
                nc.gpsimd.tensor_copy(plan[q][:, :], T["plan"][:, bass.ds(2 * t + q, 1), :]).then_inc(S[f"staged{q}"], 1)

            stage(0, 0)
            with pool.Fori(0, STEPS) as t:
                for q in range(2):
                    gather(t, q)
                    stage(*((t, 1) if q == 0 else (t + 1, 0)))
                    for i in range(ET):
                        pool.indirect_dma_start(A_cells, bass.IndirectOffsetOnAxis(ap=plan[q][:, ET + i:ET + i + 1], axis=0), plan[q][:, 2 * ET:PLAN].bitcast(U8)[:, i:i + 1], None,
                                                bounds_check=A_BYTES - 1, oob_is_err=False).then_inc(S[f"cells{q}"], 16)
            gather(STEPS, 0)
            pool.wait_ge(S["rows0"], 16 * ET * (STEPS + 1))
            for q in range(2):
                pool.wait_ge(S[f"cells{q}"], 16 * ET * STEPS)

        @blk.scalar
        def _(act):
            act.wait_ge(S["init"], 1)
            act.sem_inc(S["u_out"], 2)

            def take_u(t, q):
                for h in range(2):
                    act.wait_ge(S[f"u{q}"], 2 * t + h + 1)
                    act.wait_ge(S["z_done"], 4 * t + 2 * q + h + 1)
                    nc.scalar.activation(u[h][:, :], ps_u[h][:, :], ACT.Identity, bias=T["c2"][:, :]).then_inc(S["u_out"], 1)

            take_u(0, 0)
            with act.Fori(0, STEPS) as t:
                for q in range(2):
                    take_u(*((t, 1) if q == 0 else (t + 1, 0)))
                    act.wait_ge(S[f"m_bias{q}"], t + 1)
                    nc.scalar.activation(msg[q][:, :, 0:D], msg[q][:, :, 0:D], ACT.Tanh).then_inc(S[f"tanh{q}"], 1)

        @blk.vector
        def _(dve):
            nc.vector.memset(aggT[:, :], 0.0)
            for q in range(2):
                nc.vector.memset(msg[q][:, :, :], 1.0)

            def place_from(t, q):
                dve.wait_ge(S[f"loaded{q}"], 64 * t + 64)
                dve.wait_ge(S[f"u{q}"], 2 * t)
                nc.vector.tensor_scalar(from_node[q][:, :], dst_all[q][:, :], T["nodeid"][:, bass.ds(2 * t + q, 1)], None, ALU.is_equal).then_inc(S[f"from{q}"], 1)

            def place_to(t, q):
                g = 2 * t + q
                places = T["dloc"][:, bass.ds(g * ET, ET)].unsqueeze(2).to_broadcast([P, ET, W])
                nc.vector.tensor_tensor(to_node[q][:, :, :], T["iota_w"][:, :].unsqueeze(1).to_broadcast([P, ET, W]), places, ALU.is_equal).then_inc(S[f"to{q}"], 1)

            def add(g):
                base = base_of(dve, g - 1)
                dve.wait_ge(S["added"], g)
                there = aggT[:, bass.ds(base, W)]
                nc.vector.tensor_tensor(there, there, ps_w[0:D + 1, :], ALU.add).then_inc(S["added"], 1)

            nc.vector.memset(to_node[1][:, :, :], 0.0)
            dve.sem_inc(S["init"], 1)
            dve.sem_inc(S["z_done"], 2)
            place_from(0, 0)
            place_to(0, 0)
            with dve.Fori(0, STEPS) as t:
                for q in range(2):
                    g = 2 * t + q
                    following = (t, 1) if q == 0 else (t + 1, 0)
                    place_from(*following)
                    for h in range(2):
                        n = 4 * t + 2 * q + h
                        dve.wait_ge(S[f"loaded{q}"], 64 * t + 64)
                        dve.wait_ge(S["u_out"], n + 3)
                        dve.wait_ge(S["m_done"], n + 1)
                        nc.vector.tensor_tensor(z[h][:, :, :], u[h][:, :].unsqueeze(1).to_broadcast([P, 4, 512]), basis[q][:, :, 512 * h:512 * h + 512], ALU.mult).then_inc(S["z_done"], 1)
                    dve.wait_ge(S["m_done"], 4 * t + 2 * q + 4)
                    nc.vector.tensor_tensor(msg[q][:, :, 0:D], ps_m[q][:, :, :], T["iib1"][:, :].unsqueeze(1).to_broadcast([P, ET, D]), ALU.add).then_inc(S[f"m_bias{q}"], 1)
                    dve.wait_ge(S["summed"], g + 1)
                    place_to(*following)
                    add(g)
            dve.wait_ge(S["summed"], EGROUPS + 1)
            add(EGROUPS)

        @blk.tensor
        def _(pe):
            mm = nc.tensor.matmul
            pe.wait_ge(S["init"], 1)
            pe.sem_inc(S["m_done"], 2)

            def sum_group(q, n, before):
                pe.wait_ge(S[f"tanh{q}"], n)
                pe.wait_ge(S[f"to{q}"], n)
                pe.wait_ge(S["added"], before)
                pe.sem_inc(S["passed"], 1)
                for i in range(ET):
                    last = mm(ps_w[0:D + 1, :], msg[q][:, i, :], to_node[q][:, i, :], start=(i == 0), stop=(i == ET - 1))
                last.then_inc(S["summed"], 1)

            def join(t, q):
                pe.wait_ge(S[f"loaded{q}"], 64 * t + 64)
                pe.wait_ge(S[f"from{q}"], t + 1)
                pe.wait_ge(S[f"rows{q}"], 16 * ET * (t + 1))
                for h in range(2):
                    pe.wait_ge(S["u_out"], 4 * t + 2 * q + h + 1)
                    pe.sem_inc(S["passed"], 1)
                    mm(ps_u[h][:, :], window[q][:, :], from_node[q][:, 512 * h:512 * h + 512], start=True, stop=False)
                    for i in range(4):
                        last = mm(ps_u[h][:, i * P:(i + 1) * P], gathered[q][:, 4 * h + i, :], T["ident"][:, :], start=False, stop=(i == 3))
                    last.then_inc(S[f"u{q}"], 1)

            join(0, 0)
            with pe.Fori(0, STEPS) as t:
                for q in range(2):
                    g = 2 * t + q
                    join(*((t, 1) if q == 0 else (t + 1, 0)))
                    pe.wait_ge(S[f"m_bias{q}"], t)
                    for h in range(2):
                        pe.wait_ge(S["z_done"], 4 * t + 2 * q + h + 3)
                        pe.sem_inc(S["passed"], 1)
                        for i in range(4):
                            for k in range(4):
                                last = mm(ps_m[q][:, 4 * h + i, :], z[h][:, k, i * P:(i + 1) * P], T["M"][:, k, :], start=(k == 0), stop=(k == 3))
                        last.then_inc(S["m_done"], 1)
                    sum_group(1 - q, t + q, g)
            sum_group(1, STEPS, EGROUPS)


def after_edges(nc, T, w):
    with ExitStack() as c:
        sb = lambda n, s, d: c.enter_context(nc.sbuf_tensor(n, s, d))
        sem = lambda n: c.enter_context(nc.semaphore(n))
        sums = sb("sums", [D + 1, GC], F32)
        W2e = sb("W2e", [D + 1, D + 1], F32)
        ps_x = c.enter_context(nc.psum_tensor("ps_x", [P, 2, 512], F32))
        half = GT // 2
        x_sb, deg = T["x"], T["deg"]
        S = {n: sem("f_" + n) for n in "w0 w staged used ready read passed".split()}
        blk = c.enter_context(nc.Block())

        @blk.sync
        def _(sp):
            sp.wait_ge(S["w0"], 2)
            sp.dma_start(W2e[0:D, 0:D], w["ii_W2"]).then_inc(S["w"], 16)
            sp.dma_start(W2e[D:D + 1, 0:D], w["ii_b2"]).then_inc(S["w"], 16)

        @blk.gpsimd
        def _(pool):
            with pool.Fori(0, GROUPS) as g:
                pool.wait_ge(S["used"], 2 * g)
                nc.gpsimd.tensor_copy(sums[:, :], T["aggT"][:, bass.ds(g * GC, GC)]).then_inc(S["staged"], 1)

        @blk.vector
        def _(dve):
            nc.vector.memset(W2e[:, :], 0.0).then_inc(S["w0"], 1)
            dve.wait_ge(S["w0"], 1)
            nc.vector.memset(W2e[D:D + 1, D:D + 1], 1.0).then_inc(S["w0"], 1)
            with dve.Fori(0, GROUPS) as g:
                for b in range(2):
                    dve.wait_ge(S["used"], 2 * g + b + 1)
                    got = ps_x[:, b, 0:half * (D + 1)].rearrange("p (k d) -> p k d", k=half)
                    at = bass.ds(g * GT + b * half, half)
                    nc.vector.tensor_tensor(x_sb[:, at, :], x_sb[:, at, :], got[:, :, 0:D], ALU.add)
                    nc.vector.tensor_copy(deg[:, at], got[:, :, D]).then_inc(S["read"], 1)

        @blk.tensor
        def _(pe):
            pe.wait_ge(S["w"], 32)
            with pe.Fori(0, GROUPS) as g:
                pe.wait_ge(S["staged"], g + 1)
                for b in range(2):
                    pe.wait_ge(S["read"], 2 * g)
                    for i in range(half):
                        at = (b * half + i) * P
                        last = nc.tensor.matmul(ps_x[:, b, i * (D + 1):(i + 1) * (D + 1)], sums[:, at:at + P], W2e[:, :], start=True, stop=True)
                    last.then_inc(S["used"], 1)


GCN, LIGHT, GIN = "gcn", "light", "gin"
KINDS = [GCN, GCN, GCN, LIGHT, LIGHT, LIGHT, GIN]
TRANSPOSING = [n for n, k in enumerate(KINDS) if k != LIGHT]
NORMS = [2, 5]


def dense(nc, T, A_blocks, w, out):
    with ExitStack() as c:
        sb = lambda n, s, d: c.enter_context(nc.sbuf_tensor(n, s, d))
        sem = lambda n: c.enter_context(nc.semaphore(n))
        x_sb, ident, deg = T["x"], T["ident"], T["deg"]
        h = sb("h", [P, TILES, D], F32)
        table = [sb(f"table{i}", [P, TILES, 2 * D], F16) for i in range(2)]
        ring = [sb(f"ring{i}", [P, KC, GC], U8) for i in range(SLOTS)]
        agg = sb("agg", [P, GC], F32)
        hst = sb("hst", [P, GT, D], F32)
        hT = sb("hT", [P, GC], F32)
        rT = sb("rT", [D + 1, GC], F32)
        xc, sq, tmp, hb = (sb(n, [P, GT, D], F32) for n in ("xc", "sq", "tmp", "hb"))
        small = sb("small", [P, 4, GT], F32)
        inv1, inv2, t98 = (sb(n, [P, TILES], F32) for n in ("inv1", "inv2", "t98"))
        WHL = [sb(f"WHL{i}", [P, D], F32) for i in range(3)]
        WT = [sb(f"WT{i}", [P, D], F32) for i in range(3)]
        IHL, G1HL, G1T = (sb(n, [P, D], F32) for n in ("IHL", "G1HL", "G1T"))
        g1b, eps1 = sb("g1b", [D, 1], F32), sb("eps1", [P, 1], F32)
        G2 = sb("G2", [D + 1, D], F32)
        ps_a = c.enter_context(nc.psum_tensor("ps_a", [P, BANKS, 512], F32))
        ps_t = c.enter_context(nc.psum_tensor("ps_t", [P, 4, 512], F32))
        S = {n: sem("d_" + n) for n in "w w0 wready deg1 deg2 dve var root input a_free staged tp tp_out sums agg_out post read hidden hidden_out passed".split()}
        a_in = [sem(f"d_a_in{i}") for i in range(SLOTS)]
        half = GT // 2
        cols = [512, 512, 512, GC - 3 * 512]
        wide = [P, GT, D]
        blk = c.enter_context(nc.Block())

        @blk.sync
        def _(sp):
            sp.wait_ge(S["w0"], 1)
            for i, n in enumerate(("gcn_W1T", "gcn_W2T", "gcn_W3T")):
                for t, p0 in ((WHL[i], 0), (WHL[i], D), (WT[i], 0)):
                    sp.dma_start(t[p0:p0 + D, :], w[n]).then_inc(S["w"], 16)
            for t, p0 in ((G1HL, 0), (G1HL, D), (G1T, 0)):
                sp.dma_start(t[p0:p0 + D, :], w["gin_W1T"]).then_inc(S["w"], 16)
            sp.dma_start(g1b[:, :], w["gin_b1"]).then_inc(S["w"], 16)
            sp.dma_start(eps1[:, :], w["gin_eps"].to_broadcast([P, 1])).then_inc(S["w"], 16)
            sp.dma_start(G2[0:D, :], w["gin_W2T"]).then_inc(S["w"], 16)
            sp.dma_start(G2[D:D + 1, :], w["gin_b2"]).then_inc(S["w"], 16)
            for n in range(LAYERS):
                with sp.Fori(0, GROUPS) as g:
                    for k in range(CHUNKS):
                        sp.wait_ge(S["a_free"], (GROUPS * n + g) * CHUNKS + (k + 1))
                        sp.sem_inc(S["passed"], 1)
                        block = A_blocks[bass.ds(g, 1), :, KC * k:KC * k + KC, :].rearrange("g p k c -> p (g k) c")
                        sp.dma_start(ring[k % SLOTS][:, :, :], block).then_inc(a_in[k % SLOTS], 16)
            sp.wait_ge(S["input"], GROUPS * (LAYERS + 1))
            sp.dma_start(out[0:(TILES - 1) * P, :].rearrange("(k p) d -> p k d", p=P), x_sb[:, 0:TILES - 1, :]).then_inc(S["w"], 16)
            sp.dma_start(out[(TILES - 1) * P:N_NODES, :], x_sb[0:TAIL, TILES - 1, :]).then_inc(S["w"], 16)
            sp.wait_ge(S["w"], 16 * 18)

        @blk.gpsimd
        def _(pool):
            for j, n in enumerate(TRANSPOSING):
                pool.wait_ge(S["input"], GROUPS * (n + 1))
                with pool.Fori(0, GROUPS) as g:
                    pool.wait_ge(S["tp"], 4 * (GROUPS * j + g))
                    nc.gpsimd.tensor_copy(hst[:, :, :], h[:, bass.ds(g * GT, GT), :]).then_inc(S["staged"], 1)

        @blk.scalar
        def _(act):
            act.wait_ge(S["deg1"], 2)
            nc.scalar.activation(inv1[:, :], inv1[:, :], ACT.Sqrt).then_inc(S["deg2"], 1)
            nc.scalar.activation(inv2[:, :], inv2[:, :], ACT.Sqrt).then_inc(S["deg2"], 1)

            def root(n):
                act.wait_ge(S["var"], n)
                nc.scalar.activation(small[:, 2, :], small[:, 2, :], ACT.Sqrt, bias=T["eps"][:, :]).then_inc(S["root"], 1)

            with act.Fori(0, GROUPS) as g:
                root(g + 1)
            for n, kind in enumerate(KINDS):
                with act.Fori(0, GROUPS) as g:
                    if n in TRANSPOSING:
                        j = GROUPS * TRANSPOSING.index(n) + g
                        for b in range(4):
                            act.wait_ge(S["tp"], 4 * j + (b + 1))
                            nc.scalar.copy(hT[0:D, 512 * b:512 * b + cols[b]], ps_t[0:D, b, 0:cols[b]]).then_inc(S["tp_out"], 1)
                    for b in range(BANKS):
                        act.wait_ge(S["sums"], 4 * (GROUPS * n + g) + (b + 1))
                        nc.scalar.copy(agg[:, BC * b:BC * b + BC], ps_a[:, b, 0:BC]).then_inc(S["agg_out"], 1)
                    if kind == GIN:
                        for b in range(BANKS):
                            act.wait_ge(S["hidden"], 4 * g + b + 1)
                            nc.scalar.activation(rT[0:D, BC * b:BC * b + BC], ps_t[0:D, b, 0:BC], ACT.Relu, bias=g1b[:, :]).then_inc(S["hidden_out"], 1)
                    if n in NORMS:
                        root(GROUPS * (1 + NORMS.index(n)) + g + 1)

        @blk.vector
        def _(dve):
            ch = Chain(dve, S["dve"])
            for t in (*WT, G1T):
                nc.vector.memset(t[D:P, :], 0.0)
            nc.vector.memset(hT[D:P, :], 0.0)
            nc.vector.memset(rT[D:D + 1, :], 1.0)
            nc.vector.tensor_copy(IHL[0:D, :], ident[0:D, 0:D])
            nc.vector.tensor_scalar(IHL[D:P, :], ident[D:P, D:P], 1.0 / LO, None, ALU.mult).then_inc(S["w0"], 1)
            nc.vector.tensor_scalar(inv1[:, :], deg[:, :], 1.0, None, ALU.add).then_inc(S["deg1"], 1)
            nc.vector.tensor_scalar(inv2[:, :], deg[:, :], 1.0, None, ALU.max).then_inc(S["deg1"], 1)
            ch(nc.vector.tensor_scalar(t98[:, :], deg[:, :], 0.0, None, ALU.is_gt))
            dve.wait_ge(S["deg2"], 2)
            nc.vector.reciprocal(inv1[:, :], inv1[:, :])
            ch(nc.vector.reciprocal(inv2[:, :], inv2[:, :]))
            ch(nc.vector.tensor_tensor(inv2[:, :], inv2[:, :], t98[:, :], ALU.mult))
            dve.wait_ge(S["w"], 16 * 16)
            for t in (*WHL, G1HL):
                nc.vector.tensor_scalar(t[D:P, :], t[D:P, :], 1.0 / LO, None, ALU.mult)
            ch(nc.vector.tensor_scalar(eps1[:, :], eps1[:, :], 1.0, None, ALU.add))
            nc.vector.tensor_scalar(G1T[0:D, :], G1T[0:D, :], eps1[0:D, :], None, ALU.mult).then_inc(S["wready"], 1)

            def scaled(ch, v, inv, g):
                ch(nc.vector.tensor_tensor(tmp[:, :, :], v, inv[:, bass.ds(g * GT, GT)].unsqueeze(2).to_broadcast(wide), ALU.mult))
                return tmp[:, :, :]

            def norm(ch, at, to, n):
                dve.sem_inc(S["passed"], 1)
                ch(centre_and_scale(nc, ch, x_sb[:, at, :], xc[:, :, :], sq[:, :, :], small, to, S["var"], S["root"], n))

            def loop(start, body):
                with dve.Fori(0, GROUPS) as g:
                    step = STEPS_OF[body.__name__]
                    ch = Chain(dve, S["dve"], start + g * step)
                    body(ch, g, bass.ds(g * GT, GT))
                    dve.wait_ge(S["input"], GROUPS * loops[0] + g + 1)
                    assert ch.n == step, (body.__name__, ch.n)
                loops[0] += 1
                return start + GROUPS * step

            loops = [0]
            STEPS_OF = {"first": 9, "gcn": 4, "gcn_last": 11, "light": 4, "light_last": 9, "gin": 0}

            def first(ch, g, at):
                norm(ch, at, h[:, at, :], g + 1)
                split(nc, ch, scaled(ch, h[:, at, :], inv1, g), table[0][:, at, :], sq[:, :, :]).then_inc(S["input"], 1)

            start = loop(ch.n, first)
            for n, kind in enumerate(KINDS):
                to = table[(n + 1) % 2]

                def got(g, b):
                    dve.wait_ge(S["post"], 2 * (GROUPS * n + g) + (b + 1))
                    return ps_t[:, b, 0:half * D].rearrange("p (k d) -> p k d", k=half)

                def factor(inv, g, b):
                    return inv[:, bass.ds(g * GT + b * half, half)].unsqueeze(2).to_broadcast([P, half, D])

                def gcn(ch, g, at):
                    for b in range(2):
                        last = nc.vector.scalar_tensor_tensor(out=hb[:, b * half:(b + 1) * half, :], in0=got(g, b), scalar=0.0, in1=factor(inv1, g, b), op0=ALU.max, op1=ALU.mult)
                    last.then_inc(S["read"], 1)
                    dve.wait_ge(S["read"], GROUPS * n + g + 1)
                    ch(nc.vector.tensor_copy(h[:, at, :], hb[:, :, :]))
                    split(nc, ch, scaled(ch, hb[:, :, :], inv1, g), to[:, at, :], sq[:, :, :]).then_inc(S["input"], 1)

                def gcn_last(ch, g, at):
                    for b in range(2):
                        last = nc.vector.scalar_tensor_tensor(out=hb[:, b * half:(b + 1) * half, :], in0=got(g, b), scalar=0.0, in1=factor(inv1, g, b), op0=ALU.max, op1=ALU.mult)
                    last.then_inc(S["read"], 1)
                    dve.wait_ge(S["read"], GROUPS * n + g + 1)
                    ch(nc.vector.tensor_tensor(x_sb[:, at, :], x_sb[:, at, :], hb[:, :, :], ALU.add))
                    norm(ch, at, hb[:, :, :], GROUPS + g + 1)
                    ch(nc.vector.scalar_tensor_tensor(out=x_sb[:, at, :], in0=hb[:, :, :], scalar=0.25, in1=x_sb[:, at, :], op0=ALU.mult, op1=ALU.add))
                    split(nc, ch, scaled(ch, hb[:, :, :], inv2, g), to[:, at, :], sq[:, :, :]).then_inc(S["input"], 1)

                def light_sum(ch, g, at):
                    for b in range(2):
                        last = nc.vector.tensor_tensor(hb[:, b * half:(b + 1) * half, :], got(g, b), factor(inv2, g, b), ALU.mult)
                    last.then_inc(S["read"], 1)
                    dve.wait_ge(S["read"], GROUPS * n + g + 1)
                    ch(nc.vector.scalar_tensor_tensor(out=x_sb[:, at, :], in0=hb[:, :, :], scalar=0.25, in1=x_sb[:, at, :], op0=ALU.mult, op1=ALU.add))

                def light(ch, g, at):
                    light_sum(ch, g, at)
                    split(nc, ch, scaled(ch, hb[:, :, :], inv2, g), to[:, at, :], sq[:, :, :]).then_inc(S["input"], 1)

                def light_last(ch, g, at):
                    light_sum(ch, g, at)
                    norm(ch, at, h[:, at, :], 2 * GROUPS + g + 1)
                    split(nc, ch, h[:, at, :], to[:, at, :], sq[:, :, :]).then_inc(S["input"], 1)

                def gin(ch, g, at):
                    for b in range(2):
                        half_at = bass.ds(g * GT + b * half, half)
                        last = nc.vector.tensor_tensor(x_sb[:, half_at, :], got(g, b), x_sb[:, half_at, :], ALU.add)
                        if b:
                            last.then_inc(S["input"], 1)
                        else:
                            last.then_inc(S["read"], 1)

                body = {GCN: gcn_last if n in NORMS else gcn, LIGHT: light_last if n in NORMS else light, GIN: gin}[kind]
                start = loop(start, body)

        @blk.tensor
        def _(pe):
            mm = nc.tensor.matmul
            pe.sem_inc(S["a_free"], SLOTS)
            pe.wait_ge(S["wready"], 1)
            for n, kind in enumerate(KINDS):
                pe.wait_ge(S["input"], GROUPS * (n + 1))
                with pe.Fori(0, GROUPS) as g:
                    G = GROUPS * n + g
                    if n in TRANSPOSING:
                        pe.wait_ge(S["staged"], GROUPS * TRANSPOSING.index(n) + g + 1)
                        pe.wait_ge(S["read"] if kind != GIN else S["input"], G if kind != GIN else GROUPS * (n + 1) + g)
                        pe.sem_inc(S["passed"], 1)
                        for t in range(GT):
                            last = nc.tensor.transpose(ps_t[0:D, t // 4, (t % 4) * P:(t % 4 + 1) * P], hst[:, t, :], ident[:, :])
                            if t % 4 == 3 or t == GT - 1:
                                last.then_inc(S["tp"], 1)
                    pe.wait_ge(S["agg_out"], 4 * G)
                    for k in range(CHUNKS):
                        slot = k % SLOTS
                        uses = CHUNKS // SLOTS
                        pe.wait_ge(a_in[slot], 16 * (uses * G + (k // SLOTS + 1)))
                        pe.sem_inc(S["passed"], 1)
                        for i in range(KC):
                            first_tile, last_tile = k == 0 and i == 0, k == CHUNKS - 1 and i == KC - 1
                            for b in range(BANKS):
                                last = mm(ps_a[:, b, 0:BC], table[n % 2][:, KC * k + i, :], ring[slot][:, i, BC * b:BC * b + BC].bitcast(F8), start=first_tile, stop=last_tile)
                                if last_tile:
                                    last.then_inc(S["sums"], 1)
                        if k < CHUNKS - 1:
                            last.then_inc(S["a_free"], 1)
                    if n in TRANSPOSING:
                        pe.wait_ge(S["tp_out"], 4 * (GROUPS * TRANSPOSING.index(n) + g) + 4)
                    else:
                        pe.wait_ge(S["read"], G)
                    pe.wait_ge(S["agg_out"], 4 * G + 4)
                    pe.sem_inc(S["a_free"], 1)
                    if kind == GIN:
                        for b in range(BANKS):
                            at = slice(BC * b, BC * b + BC)
                            mm(ps_t[0:D, b, 0:BC], G1HL[:, :], agg[:, at], start=True, stop=False)
                            mm(ps_t[0:D, b, 0:BC], G1T[:, :], hT[:, at], start=False, stop=True).then_inc(S["hidden"], 1)
                        pe.wait_ge(S["hidden_out"], 4 * g + 4)
                        pe.sem_inc(S["passed"], 1)
                    for t in range(GT):
                        o = ps_t[:, t // half, (t % half) * D:(t % half + 1) * D]
                        at = slice(t * P, (t + 1) * P)
                        if kind == GCN:
                            mm(o, agg[:, at], WHL[n][:, :], start=True, stop=False)
                            last = mm(o, hT[:, at], WT[n][:, :], start=False, stop=True)
                        elif kind == LIGHT:
                            last = mm(o, agg[:, at], IHL[:, :], start=True, stop=True)
                        else:
                            last = mm(o, rT[:, at], G2[:, :], start=True, stop=True)
                        if t % half == half - 1:
                            last.then_inc(S["post"], 1)


def padded_edges(src, dst):
    after = P * SPAN + SHIFTS - N_EDGES
    i = np.arange(after, dtype=np.int32)
    lead = np.full(SHIFTS, NP - 1, np.int32)
    return (np.concatenate([lead, src, NP - 1 - i % 3]).astype(np.int32),
            np.concatenate([lead, dst, N_NODES + i // 3]).astype(np.int32))


def lay_out(x, src, dst, edge_attr_8, **w):
    flat = np.ascontiguousarray
    pad = EP - N_EDGES
    src_row, dst_row = padded_edges(src, dst)
    tiles = lambda a, v: flat(np.concatenate([a, np.full(pad, v, np.int32)]).reshape(ETILES, P).T)
    return {
        "x": x, "src_row": src_row, "dst_row": dst_row,
        "srcT": tiles(src, 0), "dstT": tiles(dst, NP - 1),
        "dst_seq": np.concatenate([np.zeros(EG, np.int32), dst, np.full(pad + EG, NP - 1, np.int32)]),
        "basisT": flat(np.concatenate([edge_attr_8, np.zeros((pad + EG, NB), np.float32)]).T),
        "pp_W1": w["L0_gnn_pp_W1"], "pp_b1": w["L0_gnn_pp_b1"].reshape(D, 1),
        "pp_W2": w["L0_gnn_pp_W2"], "pp_b2": w["L0_gnn_pp_b2"].reshape(D, 1),
        "pi_W1T": flat(w["L0_gnn_pi_W1"].reshape(2, D, D).transpose(2, 0, 1)).reshape(D, 2 * D),
        "pi_b1": w["L0_gnn_pi_b1"].reshape(D, 1), "pi_W2": w["L0_gnn_pi_W2"], "pi_b2": w["L0_gnn_pi_b2"].reshape(D, 1),
        "pi_W3T": flat(w["L0_gnn_pi_W3"].reshape(D, D, NB).transpose(1, 2, 0)),
        "ii_W1": w["L0_gnn_ii_W1"], "ii_b1": w["L0_gnn_ii_b1"].reshape(1, D),
        "ii_W2": w["L0_gnn_ii_W2"], "ii_b2": w["L0_gnn_ii_b2"].reshape(1, D),
        "gcn_W1T": flat(w["L1_gnn_W1"].T), "gcn_W2T": flat(w["L1_gnn_W2"].T), "gcn_W3T": flat(w["L1_gnn_W3"].T),
        "gin_eps": w["L3_gnn_eps"].reshape(1, 1), "gin_W1T": flat(w["L3_gnn_W1"].T), "gin_b1": w["L3_gnn_b1"].reshape(D, 1),
        "gin_W2T": flat(w["L3_gnn_W2"].T), "gin_b2": w["L3_gnn_b2"].reshape(1, D),
    }


def kernel(**inputs):
    import concourse.bacc as bacc
    from concourse.bass_utils import run_bass_kernel_spmd

    nc = bacc.Bacc("TRN2", target_bir_lowering=False, num_devices=1)
    arrays = lay_out(**{k: np.asarray(v) for k, v in inputs.items()})
    aps = {k: nc.dram_tensor("in_" + k, a.shape, mybir.dt.from_np(a.dtype), kind="ExternalInput").ap() for k, a in arrays.items()}
    out = nc.dram_tensor("out", (N_NODES, D), F32, kind="ExternalOutput").ap()
    build(nc, aps, out)
    r = run_bass_kernel_spmd(nc, [{"in_" + k: a for k, a in arrays.items()}], core_ids=[0])
    return r.results[0]["out"]
```

```python
import numpy as np
import concourse.bass as bass
from concourse import mybir
from contextlib import ExitStack

F32 = mybir.dt.float32
F16 = mybir.dt.float16
F8 = mybir.dt.float8e4
I32 = mybir.dt.int32
U8 = mybir.dt.uint8
ALU = mybir.AluOpType
ACT = mybir.ActivationFunctionType
AX = mybir.AxisListType

P = 128
D = 64
NB = 8
N_NODES = 12500
N_EDGES = 200000
TILES = -(-N_NODES // P)
NP = TILES * P
TAIL = N_NODES - (TILES - 1) * P
GROUPS = 7
GT = TILES // GROUPS
GC = GT * P
BANKS = 4
BC = GC // BANKS
LO = 2048.0

A_BYTES = GROUPS * NP * GC
KC = 2
CHUNKS = TILES // KC
SLOTS = 7

W = P
ET = 8
EG = ET * P
STEPS = 98
EGROUPS = 2 * STEPS
ETILES = EGROUPS * ET
EP = ETILES * P

SPAN = -(-N_EDGES // P)
SHIFTS = 7 * GROUPS
KW = SPAN + 2 * SHIFTS
PLAN = 2 * ET + ET // 4
assert SPAN <= EGROUPS * ET and EGROUPS * ET - SPAN < ET

LAYERS = 7


class Chain:

    def __init__(self, eng, sem, start=0):
        self.eng, self.sem, self.start, self.n = eng, sem, start, 0

    def mark(self, ins):
        ins.then_inc(self.sem, 1)
        self.n += 1

    def wait(self):
        self.eng.wait_ge(self.sem, self.start + self.n)

    def __call__(self, ins):
        self.mark(ins)
        self.wait()


def centre_and_scale(nc, ch, x, xc, sq, small, out, var_ready, root_ready, n):
    wide = [P, GT, D]
    s1, mean, s2, rstd = (small[:, i, :] for i in range(4))
    ch(nc.vector.tensor_reduce(out=s1, in_=x, op=ALU.add, axis=AX.X))
    ch(nc.vector.tensor_scalar(mean, s1, -1.0 / D, None, ALU.mult))
    ch(nc.vector.tensor_tensor(xc, x, mean.unsqueeze(2).to_broadcast(wide), ALU.add))
    ch(nc.vector.scalar_tensor_tensor(out=sq, in0=xc, scalar=1.0 / D, in1=xc, op0=ALU.mult, op1=ALU.mult))
    nc.vector.tensor_reduce(out=s2, in_=sq, op=ALU.add, axis=AX.X).then_inc(var_ready, 1)
    ch.eng.wait_ge(root_ready, n)
    ch(nc.vector.reciprocal(rstd, s2))
    return nc.vector.scalar_tensor_tensor(out=out, in0=xc, scalar=0.0,
                                          in1=rstd.unsqueeze(2).to_broadcast(wide), op0=ALU.max, op1=ALU.mult)


def split(nc, ch, v, table, tmp):
    ch(nc.vector.tensor_copy(table[:, :, 0:D], v))
    ch(nc.vector.tensor_tensor(tmp, v, table[:, :, 0:D], ALU.subtract))
    return nc.vector.tensor_scalar(table[:, :, D:2 * D], tmp, LO, None, ALU.mult)


def build(nc, w, out):
    x, srcT, dstT, src_row, dst_row, basisT = (w[n] for n in ("x", "srcT", "dstT", "src_row", "dst_row", "basisT"))
    A = nc.dram_tensor("counts", (A_BYTES,), U8, kind="Internal").ap()
    Us = nc.dram_tensor("u_source", (NP, 2 * D), F32, kind="Internal").ap()
    Ud = nc.dram_tensor("u_target", (NP + W, 2 * D), F32, kind="Internal").ap()
    messages = nc.dram_tensor("messages", (EP, D + 1), F32, kind="Internal").ap()
    rows16 = nc.dram_tensor("feature_rows", (NP, D), F32, kind="Internal").ap()
    irregular = nc.dram_tensor("irregular", (1, 1), I32, kind="Internal").ap()
    G = {"messages": messages, "rows": rows16, "irregular": irregular, "src": srcT, "dst": dstT}
    A_cells = A.rearrange("(n a) -> n a", a=1)
    A_blocks = A.rearrange("(g p k c) -> g p k c", g=GROUPS, p=P, k=TILES)
    A_flat = A.rearrange("(p n) -> p n", p=P)

    with ExitStack() as ctx:
        sb = lambda n, s, d: ctx.enter_context(nc.sbuf_tensor(n, s, d))
        sem = lambda n: ctx.enter_context(nc.semaphore(n))
        T = {}
        T["x"] = sb("x_sb", [P, TILES, D], F32)
        T["ident"] = sb("ident", [P, P], F32)
        T["M"] = sb("M_sb", [P, 4, D], F32)
        T["c2"] = sb("c2", [P, 1], F32)
        T["iib1"] = sb("iib1", [P, D], F32)
        T["ones"] = sb("ones", [1, P], F32)
        T["nodeid"] = sb("nodeid", [P, EGROUPS + 1], F32)
        T["eps"] = sb("eps", [P, 1], F32)
        T["deg"] = sb("deg", [P, TILES], F32)
        T["iota_w"] = sb("iota_w", [P, W], F32)
        T["group_base"] = sb("group_base", [P, GROUPS], F32)
        with ExitStack() as edge:
            esb = lambda n, s, d: edge.enter_context(nc.sbuf_tensor(n, s, d))
            T["plan"] = esb("plan", [P, EGROUPS + 1, PLAN], I32)
            T["dloc"] = esb("dloc", [P, ETILES + ET], F32)
            zero = esb("zero", [P, 12544], U8)
            zeroed = [sem("zeroed0"), sem("zeroed1")]
            T["zeroed"] = zeroed
            prepare(nc, ctx, T, A_flat, zero, zeroed, x, srcT, dstT, src_row, dst_row, w, Us, Ud, irregular)
            T["aggT"] = esb("aggT", [D + 1, NP + W], F32)
            T["zero"] = zero
            edges(nc, ctx, T, A_cells, Us, Ud, w, G)
            after_edges(nc, T, w)
        dense(nc, T, A_blocks, w, out, G)


def prepare(nc, ctx, T, A_flat, zero, zeroed, x, srcT, dstT, src_row, dst_row, w, Us, Ud, irregular):
    with ExitStack() as c:
        sb = lambda n, s, d: c.enter_context(nc.sbuf_tensor(n, s, d))
        ps = lambda n, s: c.enter_context(nc.psum_tensor(n, s, F32))
        sem = lambda n: c.enter_context(nc.semaphore(n))
        x_sb, ident = T["x"], T["ident"]
        sA, dA = sb("sA", [P, KW], I32), sb("dA", [P, KW], I32)
        key = sb("key", [P, KW], I32)
        t1, t2, gidx = sb("t1", [P, KW], I32), sb("t2", [P, KW], I32), sb("gidx", [P, KW], I32)
        later, earlier = sb("later", [P, SPAN], F32), sb("earlier", [P, SPAN], F32)
        dT = sb("dT", [P, ETILES], I32)
        count = sb("count", [P, SPAN + 1], F8)
        faults = sb("faults", [P, 6], F32)
        fault_row = sb("fault_row", [1, 1], I32)
        base_row = sb("base_row", [1, EGROUPS], F32)
        base_bc = sb("base_bc", [P, EGROUPS], F32)
        iota_i = sb("iota_i", [P, W + 1], I32)
        iota_p = sb("iota_p", [P, 1], F32)
        xc, sq, hst = (sb(n, [P, GT, D], F32) for n in ("xc0", "sq0", "hst0"))
        small = sb("small0", [P, 4, GT], F32)
        hT, t1T, p1T = (sb(n, [D, GC], F32) for n in ("hT0", "t1T", "p1T"))
        us, ud = sb("us", [P, GT, 2, D], F32), sb("ud", [P, GT, 2, D], F32)
        ppW1, ppW2, piW2, iiW1 = (sb(n, [D, D], F32) for n in ("ppW1", "ppW2", "piW2", "iiW1"))
        piW1T = sb("piW1T", [D, 2 * D], F32)
        piW2d = sb("piW2d", [D, 2, D], F32)
        W3T = sb("W3T", [D, NB, D], F32)
        ppb1, ppb2, pib1 = (sb(n, [D, 1], F32) for n in ("ppb1", "ppb2", "pib1"))
        pib2 = sb("pib2", [P, 1], F32)
        Cab = sb("Cab", [D, 2 * D], F32)
        psA = ps("psA", [P, 4, 512])
        psB = ps("psB", [P, 4, 512])

        S = {n: sem("p_" + n) for n in (
            "x keys plan0 srcT dT w iotas id0 ident dve wts wtsdone base basebc h_ready tp tp_ev z1 z1_ev z2 z2_ev tb tb_ev st zinit var root eps faults faultsum fault_out passed".split())}
        n_weights = 12
        blk = c.enter_context(nc.Block())

        @blk.sync
        def _(sp):
            sp.dma_start(x_sb[:, 0:TILES - 1, :], x[0:(TILES - 1) * P, :].rearrange("(k p) d -> p k d", p=P)).then_inc(S["x"], 16)
            sp.wait_ge(S["zinit"], 2)
            sp.dma_start(x_sb[0:TAIL, TILES - 1, :], x[(TILES - 1) * P:N_NODES, :]).then_inc(S["x"], 16)
            for r, t in ((src_row, sA), (dst_row, dA)):
                lap = bass.AP(tensor=r.tensor, offset=r.offset, ap=[[SPAN, P], [1, KW]])
                sp.dma_start(t[:, :], lap).then_inc(S["keys"], 16)
            sp.wait_ge(S["plan0"], 1)
            sp.dma_start(T["plan"][:, 0:EGROUPS, 0:ET], srcT.rearrange("p (g t) -> p g t", t=ET)).then_inc(S["srcT"], 16)
            sp.dma_start(dT[:, :], dstT).then_inc(S["dT"], 16)
            with sp.Fori(0, GROUPS) as g:
                sp.wait_ge(S["tb_ev"], 4 * g + 4)
                sp.dma_start(Us.rearrange("(k p) d -> p k d", p=P)[:, bass.ds(g * GT, GT), :], us[:, :, :, :].rearrange("p k h d -> p k (h d)")).then_inc(S["st"], 16)
                sp.dma_start(Ud[0:NP, :].rearrange("(k p) d -> p k d", p=P)[:, bass.ds(g * GT, GT), :], ud[:, :, :, :].rearrange("p k h d -> p k (h d)")).then_inc(S["st"], 16)
            sp.dma_start(Ud[NP:NP + W, :], x_sb[:, 0:2, :].rearrange("p k d -> p (k d)")).then_inc(S["st"], 16)
            sp.wait_ge(S["st"], 16 * (2 * GROUPS + 1))
            sp.wait_ge(S["srcT"], 16)
            sp.wait_ge(S["fault_out"], 1)
            sp.dma_start(irregular, fault_row[:, :]).then_inc(S["st"], 16)
            sp.wait_ge(S["st"], 16 * (2 * GROUPS + 2))

        @blk.gpsimd
        def _(pool):
            nc.gpsimd.memset(zero[:, :], 0).then_inc(S["zinit"], 1)
            nc.gpsimd.memset(x_sb[:, TILES - 1, :], 0.0).then_inc(S["zinit"], 1)
            nc.gpsimd.memset(ident[:, :], 0.0).then_inc(S["id0"], 1)
            pool.wait_ge(S["id0"], 1)
            pool.affine_select(out=ident[:, :], in_=ident[:, :], compare_op=ALU.not_equal, fill=1.0,
                               base=0, pattern=[[-1, P]], channel_multiplier=1).then_inc(S["ident"], 1)
            nc.gpsimd.iota(iota_i[:, 0:W], pattern=[[1, W]], base=0, channel_multiplier=0).then_inc(S["iotas"], 1)
            nc.gpsimd.iota(iota_i[:, W:W + 1], pattern=[[0, 1]], base=0, channel_multiplier=1).then_inc(S["iotas"], 1)
            pool.wait_ge(S["zinit"], 2)
            pool.wait_ge(S["x"], 32)
            pool.wait_ge(S["keys"], 32)
            pool.wait_ge(S["dT"], 16)
            width = zero.shape[1]
            def fill(i, q):
                pool.dma_start(A_flat[:, bass.ds((2 * i + q) * width, width)], zero[:, :]).then_inc(zeroed[q], 16)

            fill(0, 0)
            fill(0, 1)
            with pool.Fori(0, A_BYTES // P // width // 2 - 1) as i:
                for q in range(2):
                    pool.wait_ge(zeroed[q], 16 * i + 16)
                    pool.sem_inc(S["passed"], 1)
                    fill(i + 1, q)

        @blk.scalar
        def _(act):
            loads = [(ppW1[:, :], w["pp_W1"]), (ppW2[:, :], w["pp_W2"]), (piW2[:, :], w["pi_W2"]), (iiW1[:, :], w["ii_W1"]),
                     (piW1T[:, :], w["pi_W1T"]), (W3T[:, :, :], w["pi_W3T"]),
                     (ppb1[:, :], w["pp_b1"]), (ppb2[:, :], w["pp_b2"]), (pib1[:, :], w["pi_b1"]),
                     (pib2[0:D, :], w["pi_b2"]), (pib2[D:P, :], w["pi_b2"]), (T["iib1"][:, :], w["ii_b1"].to_broadcast([P, D]))]
            assert len(loads) == n_weights
            for t, a in loads:
                act.dma_start(t, a).then_inc(S["w"], 16)
            act.wait_ge(S["w"], 16 * n_weights)
            act.wait_ge(S["dve"], 1)
            act.wait_ge(S["wts"], 1)
            nc.scalar.copy(Cab[:, :], psA[0:D, 0, 0:2 * D])
            nc.scalar.activation(T["c2"][:, :], psA[:, 1, 0:1], ACT.Identity, bias=pib2[:, :])
            nc.scalar.copy(T["M"][:, :, :], psA[:, 2, 0:4 * D].rearrange("p (c m) -> p c m", c=4)).then_inc(S["wtsdone"], 1)
            cols = [512, 512, 512, GC - 3 * 512]
            act.wait_ge(S["eps"], 1)
            with act.Fori(0, GROUPS) as g:
                act.wait_ge(S["var"], g + 1)
                nc.scalar.activation(small[:, 2, :], small[:, 2, :], ACT.Sqrt, bias=T["eps"][:, :]).then_inc(S["root"], 1)
                for b in range(4):
                    act.wait_ge(S["tp"], 4 * g + b + 1)
                    nc.scalar.copy(hT[:, 512 * b:512 * b + cols[b]], psA[0:D, b, 0:cols[b]]).then_inc(S["tp_ev"], 1)
                for b in range(4):
                    act.wait_ge(S["z1"], 4 * g + b + 1)
                    nc.scalar.activation(t1T[:, BC * b:BC * b + BC], psB[0:D, b, 0:BC], ACT.Tanh, bias=ppb1[:, :]).then_inc(S["z1_ev"], 1)
                for b in range(4):
                    act.wait_ge(S["z2"], 4 * g + b + 1)
                    nc.scalar.activation(p1T[:, BC * b:BC * b + BC], psA[0:D, b, 0:BC], ACT.Identity, bias=ppb2[:, :]).then_inc(S["z2_ev"], 1)
                act.wait_ge(S["st"], 32 * g)
                for b in range(4):
                    act.wait_ge(S["tb"], 4 * g + b + 1)
                    n = cols[b] // P
                    v = psB[:, b, 0:cols[b]].rearrange("p (k h d) -> p k h d", h=2, d=D)
                    twice = [P, n, 2, D]
                    nc.scalar.copy(us[:, 4 * b:4 * b + n, :, :], v[:, :, 0, :].unsqueeze(2).to_broadcast(twice))
                    nc.scalar.copy(ud[:, 4 * b:4 * b + n, :, :], v[:, :, 1, :].unsqueeze(2).to_broadcast(twice)).then_inc(S["tb_ev"], 1)

        @blk.vector
        def _(dve):
            ch = Chain(dve, S["dve"])
            nc.vector.memset(T["ones"][:, :], 1.0)
            for g in range(GROUPS):
                nc.vector.memset(T["group_base"][:, g:g + 1], float(GC * g))
            nc.vector.memset(T["eps"][:, :], 1e-5).then_inc(S["eps"], 1)
            nc.vector.memset(T["nodeid"][:, EGROUPS:EGROUPS + 1], -1.0)
            nc.vector.memset(T["dloc"][:, ETILES:ETILES + ET], -1.0)
            nc.vector.memset(T["plan"][:, :, :], 0).then_inc(S["plan0"], 1)
            nc.vector.memset(later[:, :], 0.0)
            nc.vector.memset(earlier[:, :], 0.0)
            dve.wait_ge(S["plan0"], 1)
            nc.vector.memset(T["plan"][:, EGROUPS - 1:EGROUPS + 1, ET:2 * ET], 1 << 29)
            dve.wait_ge(S["w"], 16 * n_weights)
            ch(nc.vector.tensor_copy(piW2d[:, :, :], piW2[:, :].unsqueeze(1).to_broadcast([D, 2, D])))
            dve.wait_ge(S["keys"], 32)
            ch(nc.vector.tensor_scalar(gidx[:, :], dA[:, :], GC, None, ALU.is_ge))
            for i in range(2, GROUPS):
                ch(nc.vector.scalar_tensor_tensor(out=gidx[:, :], in0=dA[:, :], scalar=float(GC * i), in1=gidx[:, :], op0=ALU.is_ge, op1=ALU.add))
            nc.vector.tensor_scalar(t1[:, :], sA[:, :], 127, None, ALU.bitwise_and)
            ch(nc.vector.tensor_scalar(t2[:, :], sA[:, :], 7, None, ALU.logical_shift_right))
            ch(nc.vector.scalar_tensor_tensor(out=t1[:, :], in0=t1[:, :], scalar=float(TILES), in1=t2[:, :], op0=ALU.mult, op1=ALU.add))
            ch(nc.vector.tensor_scalar(t2[:, :], dA[:, :], 7, None, ALU.logical_shift_right))
            ch(nc.vector.scalar_tensor_tensor(out=t1[:, :], in0=t1[:, :], scalar=float(GT), in1=t2[:, :], op0=ALU.mult, op1=ALU.add))
            ch(nc.vector.scalar_tensor_tensor(out=t1[:, :], in0=gidx[:, :], scalar=float((NP - 1) * GT), in1=t1[:, :], op0=ALU.mult, op1=ALU.add))
            nc.vector.tensor_scalar(t2[:, :], dA[:, :], 127, None, ALU.bitwise_and)
            ch(nc.vector.tensor_scalar(t1[:, :], t1[:, :], 7, None, ALU.logical_shift_left))
            ch(nc.vector.tensor_tensor(key[:, :], t1[:, :], t2[:, :], ALU.bitwise_or))
            dve.wait_ge(S["dT"], 16)
            dve.wait_ge(S["iotas"], 2)
            nc.vector.tensor_copy(base_row[:, :], dT[0:1, :].rearrange("p (g t) -> p g t", t=ET)[:, :, 0]).then_inc(S["base"], 1)
            nc.vector.tensor_copy(T["iota_w"][:, :], iota_i[:, 0:W])
            ch(nc.vector.tensor_copy(iota_p[:, :], iota_i[:, W:W + 1]))
            dve.wait_ge(S["basebc"], 1)
            ch(nc.vector.tensor_copy(base_bc[:, :], psB[:, 0, 0:EGROUPS]))
            nc.vector.tensor_scalar(T["nodeid"][:, 0:EGROUPS], base_bc[:, :], iota_p[:, :], None, ALU.add)
            ch(nc.vector.tensor_tensor(T["dloc"][:, 0:ETILES].rearrange("p (g t) -> p g t", t=ET), dT[:, :].rearrange("p (g t) -> p g t", t=ET),
                                       base_bc[:, :].unsqueeze(2).to_broadcast([P, EGROUPS, ET]), ALU.subtract))
            dve.wait_ge(S["x"], 32)
            dve.wait_ge(S["zinit"], 2)
            before = ch.n
            step = 5 + 3 * (SHIFTS // GROUPS)
            reach = SPAN + SHIFTS
            diffs = (t1, t2)
            with dve.Fori(0, GROUPS) as g:
                ch = Chain(dve, S["dve"], before + g * step)
                dve.wait_ge(S["tp"], 4 * g)
                centre_and_scale(nc, ch, x_sb[:, bass.ds(g * GT, GT), :], xc[:, :, :], sq[:, :, :], small, hst[:, :, :],
                                 S["var"], S["root"], g + 1).then_inc(S["h_ready"], 1)
                for u in range(SHIFTS // GROUPS):
                    s = g * (SHIFTS // GROUPS) + (u + 1)
                    diff = diffs[u % 2]
                    ch(nc.vector.tensor_tensor(diff[:, 0:reach], key[:, 0:reach], key[:, bass.ds(s, reach)], ALU.bitwise_xor))
                    ch.mark(nc.vector.scalar_tensor_tensor(out=later[:, :], in0=diff[:, SHIFTS:reach], scalar=0.0, in1=later[:, :], op0=ALU.is_equal, op1=ALU.add))
                    ch.mark(nc.vector.scalar_tensor_tensor(out=earlier[:, :], in0=diff[:, bass.ds(SHIFTS - s, SPAN)], scalar=0.0, in1=earlier[:, :], op0=ALU.is_equal, op1=ALU.add))
                ch.wait()
                assert ch.n == step, ch.n
            ch = Chain(dve, S["dve"], before + GROUPS * step)
            full = SPAN // ET
            nc.vector.tensor_scalar(count[:, 0:SPAN], later[:, :], 1.0, None, ALU.add, saturate=False)
            ch(nc.vector.tensor_scalar(t2[:, 0:SPAN], earlier[:, :], 0.0, float(1 << 29), ALU.is_gt, ALU.mult))
            for groups, at, n in ((slice(0, full), slice(0, full * ET), ET), (slice(full, full + 1), slice(full * ET, SPAN), SPAN - full * ET)):
                cut = lambda a: a[:, at].rearrange("p (g t) -> p g t", t=n)
                keys = key[:, SHIFTS + at.start:SHIFTS + at.stop].rearrange("p (g t) -> p g t", t=n)
                nc.vector.tensor_tensor(T["plan"][:, groups, ET:ET + n], keys, cut(t2), ALU.bitwise_or)
                counts = T["plan"][:, groups, 2 * ET:PLAN].bitcast(U8)[:, :, 0:n]
                ch(nc.vector.tensor_copy(counts, cut(count).bitcast(U8)))
            own = slice(SHIFTS, SHIFTS + SPAN)
            ch(nc.vector.tensor_tensor(t1[:, 0:SPAN], dA[:, SHIFTS + 1:SHIFTS + 1 + SPAN], dA[:, own], ALU.is_lt))
            ch(nc.vector.tensor_reduce(out=faults[:, 0:1], in_=t1[:, 0:SPAN], op=ALU.max, axis=AX.X))
            ch(nc.vector.tensor_tensor(t1[:, 0:SPAN], dA[:, 2 * SHIFTS:2 * SHIFTS + SPAN], dA[:, own], ALU.is_equal))
            ch(nc.vector.tensor_reduce(out=faults[:, 1:2], in_=t1[:, 0:SPAN], op=ALU.max, axis=AX.X))
            ch(nc.vector.tensor_reduce(out=faults[:, 2:3], in_=later[:, :], op=ALU.max, axis=AX.X))
            ch(nc.vector.tensor_scalar(faults[:, 2:3], faults[:, 2:3], 15.0, None, ALU.is_gt))
            ch(nc.vector.tensor_reduce(out=faults[:, 3:4], in_=T["dloc"][:, 0:ETILES], op=ALU.max, axis=AX.X))
            ch(nc.vector.tensor_scalar(faults[:, 3:4], faults[:, 3:4], float(W - 1), None, ALU.is_gt))
            ch(nc.vector.tensor_reduce(out=faults[:, 4:5], in_=faults[:, 0:4], op=ALU.add, axis=AX.X))
            nc.vector.memset(faults[:, 5:6], 1.0).then_inc(S["faults"], 1)
            dve.wait_ge(S["faultsum"], 1)
            nc.vector.tensor_scalar(fault_row[:, :], psB[0:1, 0, 0:1], 0.0, None, ALU.is_gt).then_inc(S["fault_out"], 1)

        @blk.tensor
        def _(pe):
            pe.wait_ge(S["dve"], 1)
            pe.wait_ge(S["w"], 16 * n_weights)
            mm = nc.tensor.matmul
            mm(psA[0:D, 0, 0:D], piW1T[:, 0:D], piW2[:, :], start=True, stop=True)
            mm(psA[0:D, 0, D:2 * D], piW1T[:, D:2 * D], piW2[:, :], start=True, stop=True)
            mm(psA[:, 1, 0:1], piW2d[:, :, :], pib1[:, :], start=True, stop=True)
            for q in range(4):
                last = mm(psA[:, 2, q * D:(q + 1) * D], W3T[:, 2 * q:2 * q + 2, :], iiW1[:, :], start=True, stop=True)
            last.then_inc(S["wts"], 1)
            pe.wait_ge(S["base"], 1)
            mm(psB[:, 0, 0:EGROUPS], T["ones"][:, :], base_row[:, :], start=True, stop=True).then_inc(S["basebc"], 1)
            pe.wait_ge(S["ident"], 1)
            pe.wait_ge(S["wtsdone"], 1)
            with pe.Fori(0, GROUPS) as g:
                pe.wait_ge(S["h_ready"], g + 1)
                pe.wait_ge(S["z2_ev"], 4 * g)
                pe.sem_inc(S["passed"], 1)
                for t in range(GT):
                    last = nc.tensor.transpose(psA[0:D, t // 4, (t % 4) * P:(t % 4 + 1) * P], hst[:, t, :], ident[:, :])
                    if t % 4 == 3 or t == GT - 1:
                        last.then_inc(S["tp"], 1)
                pe.wait_ge(S["tb_ev"], 4 * g)
                for b in range(4):
                    pe.wait_ge(S["tp_ev"], 4 * g + min(b + 1, 4))
                    pe.sem_inc(S["passed"], 1)
                    mm(psB[0:D, b, 0:BC], ppW1[:, :], hT[:, BC * b:BC * b + BC], start=True, stop=True).then_inc(S["z1"], 1)
                for b in range(4):
                    pe.wait_ge(S["z1_ev"], 4 * g + b + 1)
                    pe.sem_inc(S["passed"], 1)
                    mm(psA[0:D, b, 0:BC], ppW2[:, :], t1T[:, BC * b:BC * b + BC], start=True, stop=True).then_inc(S["z2"], 1)
                for t in range(GT):
                    if t % 4 == 0:
                        pe.wait_ge(S["z2_ev"], 4 * g + min(t // 4 + 2, 4))
                        pe.sem_inc(S["passed"], 1)
                    last = mm(psB[:, t // 4, (t % 4) * P:(t % 4 + 1) * P], p1T[:, t * P:(t + 1) * P], Cab[:, :], start=True, stop=True)
                    if t % 4 == 3 or t == GT - 1:
                        last.then_inc(S["tb"], 1)
            pe.wait_ge(S["faults"], 1)
            pe.wait_ge(S["tb_ev"], 4 * GROUPS)
            pe.sem_inc(S["passed"], 1)
            mm(psB[0:1, 0, 0:1], faults[:, 4:5], faults[:, 5:6], start=True, stop=True).then_inc(S["faultsum"], 1)


def edges(nc, ctx, T, A_cells, Us, Ud, w, G):
    dst_seq, basisT = w["dst_seq"], w["basisT"]
    with ExitStack() as c:
        sb = lambda n, s, d: c.enter_context(nc.sbuf_tensor(n, s, d))
        ps = lambda n, s: c.enter_context(nc.psum_tensor(n, s, F32))
        sem = lambda n: c.enter_context(nc.semaphore(n))
        two = lambda f, n, *a: [f(f"{n}{q}", *a) for q in range(2)]
        basis = two(sb, "basis", [P, 4, EG], F32)
        dst_all = two(sb, "dst_all", [P, EG], I32)
        window = two(sb, "window", [P, 2 * D], F32)
        from_node = two(sb, "from_node", [P, EG], F32)
        to_node = two(sb, "to_node", [P, ET, W], F32)
        gathered = two(sb, "gathered", [P, ET, 2 * D], F32)
        u = two(sb, "u", [P, 512], F32)
        z = two(sb, "z", [P, 4, 512], F32)
        msg = two(sb, "msg", [P, ET, D + 1], F32)
        plan = two(sb, "plan_now", [P, PLAN], I32)
        ps_u = two(ps, "ps_u", [P, 512])
        ps_m = two(ps, "ps_m", [P, ET, D])
        ps_w = ps("ps_w", [P, W])
        aggT = T["aggT"]
        S = {n: sem("e_" + n) for n in "init staged0 staged1 from0 from1 to0 to1 loaded0 loaded1 rows0 rows1 cells0 cells1 u0 u1 u_out z_done m_done m_bias0 m_bias1 tanh0 tanh1 summed added passed".split()}
        messages = G["messages"]
        ends = sb("ends", [P, 2, ET], I32)
        target = sb("target", [P, ET], I32)
        place = sb("place", [P, ET], F32)
        places = basis[1][:, :, :].rearrange("p b e -> p (b e)")[:, 0:GC]
        hot = [t[:, :, :].rearrange("p b e -> p (b e)")[:, 0:GC] for t in z]
        banks = [t[:, :] for t in ps_u] + [t[:, :, :].rearrange("p t d -> p (t d)") for t in ps_m]
        V = {n: sem("v_" + n) for n in "dve basis ends rows u u_out z m bias tanh stored back placed hot used taken".split()}
        blk = c.enter_context(nc.Block())

        def choose(eng, regular, general):
            flag = eng.value_load(G["irregular"], min_val=0, max_val=1)
            with eng.If(flag < 1):
                regular(eng)
            with eng.Else():
                general(eng)

        def load_basis(eng, g, q, signal):
            for h in range(2):
                rows = basisT[h:NB:2, bass.ds(g * EG, EG)]
                rows = bass.AP(tensor=rows.tensor, offset=rows.offset, ap=[[0, D]] + [list(a) for a in rows.ap])
                eng.dma_start(basis[q][h * D:(h + 1) * D, :, :], rows).then_inc(signal, 16)

        base_of = lambda eng, g: eng.value_load(dst_seq[bass.ds((g + 1) * EG, 1)].unsqueeze(0), min_val=0, max_val=NP - 1)

        @blk.sync
        def _(sp):
            def regular(sp):
                def load(t, q):
                    g = 2 * t + q
                    base = base_of(sp, g)
                    sp.wait_ge(S["z_done"], 4 * t + 2 * q)
                    load_basis(sp, g, q, S[f"loaded{q}"])
                    sp.dma_start(dst_all[q][:, :], dst_seq[bass.ds((g + 1) * EG, EG)].unsqueeze(0).to_broadcast([P, EG])).then_inc(S[f"loaded{q}"], 16)
                    sp.dma_start(window[q][:, :], Ud[bass.ds(base, W), :]).then_inc(S[f"loaded{q}"], 16)

                with sp.Fori(0, STEPS) as t:
                    for q in range(2):
                        load(t, q)
                load(STEPS, 0)
                sp.wait_ge(S["loaded0"], 64 * (STEPS + 1))

            def general(sp):
                with sp.Fori(0, EGROUPS) as g:
                    sp.wait_ge(V["z"], 2 * g)
                    sp.sem_inc(S["passed"], 1)
                    load_basis(sp, g, 0, V["basis"])
                    sp.wait_ge(V["tanh"], g + 1)
                    sp.sem_inc(S["passed"], 1)
                    at = messages[bass.ds(g * EG, EG), :].rearrange("(t p) d -> p t d", p=P)
                    sp.dma_start(at, msg[0][:, :, :]).then_inc(V["stored"], 16)
                sp.wait_ge(V["stored"], 16 * EGROUPS)
                with sp.Fori(0, GROUPS) as group:
                    with sp.Fori(0, EGROUPS) as g:
                        n = group * EGROUPS + g
                        sp.wait_ge(V["used"], ET * n)
                        sp.sem_inc(S["passed"], 1)
                        at = messages[bass.ds(g * EG, EG), :].rearrange("(t p) d -> p t d", p=P)
                        sp.dma_start(msg[0][:, :, :], at).then_inc(V["back"], 16)
                        sp.dma_start(target[:, :], G["dst"][:, bass.ds(g * ET, ET)]).then_inc(V["back"], 16)

            choose(sp, regular, general)

        @blk.gpsimd
        def _(pool):
            def regular(pool):
                for z0 in T["zeroed"]:
                    pool.wait_ge(z0, 16 * (A_BYTES // P // T["zero"].shape[1] // 2))

                def gather(t, q):
                    pool.wait_ge(S[f"u{q}"], 2 * t)
                    pool.wait_ge(S[f"staged{q}"], t + 1)
                    pool.sem_inc(S["passed"], 1)
                    for i in range(ET):
                        pool.indirect_dma_start(gathered[q][:, i, :], None, Us, bass.IndirectOffsetOnAxis(ap=plan[q][:, i:i + 1], axis=0)).then_inc(S[f"rows{q}"], 16)

                def stage(t, q):
                    pool.wait_ge(S[f"rows{q}"], 16 * ET * t)
                    pool.wait_ge(S[f"cells{q}"], 16 * ET * t)
                    pool.sem_inc(S["passed"], 1)
                    nc.gpsimd.tensor_copy(plan[q][:, :], T["plan"][:, bass.ds(2 * t + q, 1), :]).then_inc(S[f"staged{q}"], 1)

                stage(0, 0)
                with pool.Fori(0, STEPS) as t:
                    for q in range(2):
                        gather(t, q)
                        stage(*((t, 1) if q == 0 else (t + 1, 0)))
                        for i in range(ET):
                            pool.indirect_dma_start(A_cells, bass.IndirectOffsetOnAxis(ap=plan[q][:, ET + i:ET + i + 1], axis=0), plan[q][:, 2 * ET:PLAN].bitcast(U8)[:, i:i + 1], None,
                                                    bounds_check=A_BYTES - 1, oob_is_err=False).then_inc(S[f"cells{q}"], 16)
                gather(STEPS, 0)
                pool.wait_ge(S["rows0"], 16 * ET * (STEPS + 1))
                for q in range(2):
                    pool.wait_ge(S[f"cells{q}"], 16 * ET * STEPS)

            def general(pool):
                with pool.Fori(0, EGROUPS) as g:
                    pool.wait_ge(V["u"], 2 * g)
                    pool.sem_inc(S["passed"], 1)
                    pool.dma_start(ends[:, 0, :], G["src"][:, bass.ds(g * ET, ET)]).then_inc(V["ends"], 16)
                    pool.dma_start(ends[:, 1, :], G["dst"][:, bass.ds(g * ET, ET)]).then_inc(V["ends"], 16)
                    pool.wait_ge(V["ends"], 32 * g + 32)
                    pool.sem_inc(S["passed"], 1)
                    for end, nodes in enumerate((Us, Ud)):
                        for i in range(ET):
                            pool.indirect_dma_start(gathered[end][:, i, :], None, nodes, bass.IndirectOffsetOnAxis(ap=ends[:, end, i:i + 1], axis=0)).then_inc(V["rows"], 16)
                pool.wait_ge(V["rows"], 32 * ET * EGROUPS)

            choose(pool, regular, general)

        @blk.scalar
        def _(act):
            def regular(act):
                act.wait_ge(S["init"], 1)
                act.sem_inc(S["u_out"], 2)

                def take_u(t, q):
                    for h in range(2):
                        act.wait_ge(S[f"u{q}"], 2 * t + h + 1)
                        act.wait_ge(S["z_done"], 4 * t + 2 * q + h + 1)
                        nc.scalar.activation(u[h][:, :], ps_u[h][:, :], ACT.Identity, bias=T["c2"][:, :]).then_inc(S["u_out"], 1)

                take_u(0, 0)
                with act.Fori(0, STEPS) as t:
                    for q in range(2):
                        take_u(*((t, 1) if q == 0 else (t + 1, 0)))
                        act.wait_ge(S[f"m_bias{q}"], t + 1)
                        nc.scalar.activation(msg[q][:, :, 0:D], msg[q][:, :, 0:D], ACT.Tanh).then_inc(S[f"tanh{q}"], 1)

            def general(act):
                with act.Fori(0, EGROUPS) as g:
                    for h in range(2):
                        act.wait_ge(V["u"], 2 * g + h + 1)
                        act.wait_ge(V["z"], 2 * g)
                        nc.scalar.activation(u[h][:, :], ps_u[h][:, :], ACT.Identity, bias=T["c2"][:, :]).then_inc(V["u_out"], 1)
                    act.wait_ge(V["bias"], g + 1)
                    nc.scalar.activation(msg[0][:, :, 0:D], msg[0][:, :, 0:D], ACT.Tanh).then_inc(V["tanh"], 1)

            choose(act, regular, general)

        @blk.vector
        def _(dve):
            def regular(dve):
                nc.vector.memset(aggT[:, :], 0.0)
                for q in range(2):
                    nc.vector.memset(msg[q][:, :, :], 1.0)

                def place_from(t, q):
                    dve.wait_ge(S[f"loaded{q}"], 64 * t + 64)
                    dve.wait_ge(S[f"u{q}"], 2 * t)
                    nc.vector.tensor_scalar(from_node[q][:, :], dst_all[q][:, :], T["nodeid"][:, bass.ds(2 * t + q, 1)], None, ALU.is_equal).then_inc(S[f"from{q}"], 1)

                def place_to(t, q):
                    g = 2 * t + q
                    places = T["dloc"][:, bass.ds(g * ET, ET)].unsqueeze(2).to_broadcast([P, ET, W])
                    nc.vector.tensor_tensor(to_node[q][:, :, :], T["iota_w"][:, :].unsqueeze(1).to_broadcast([P, ET, W]), places, ALU.is_equal).then_inc(S[f"to{q}"], 1)

                def add(g):
                    base = base_of(dve, g - 1)
                    dve.wait_ge(S["added"], g)
                    there = aggT[:, bass.ds(base, W)]
                    nc.vector.tensor_tensor(there, there, ps_w[0:D + 1, :], ALU.add).then_inc(S["added"], 1)

                nc.vector.memset(to_node[1][:, :, :], 0.0)
                dve.sem_inc(S["init"], 1)
                dve.sem_inc(S["z_done"], 2)
                place_from(0, 0)
                place_to(0, 0)
                with dve.Fori(0, STEPS) as t:
                    for q in range(2):
                        g = 2 * t + q
                        following = (t, 1) if q == 0 else (t + 1, 0)
                        place_from(*following)
                        for h in range(2):
                            n = 4 * t + 2 * q + h
                            dve.wait_ge(S[f"loaded{q}"], 64 * t + 64)
                            dve.wait_ge(S["u_out"], n + 3)
                            dve.wait_ge(S["m_done"], n + 1)
                            nc.vector.tensor_tensor(z[h][:, :, :], u[h][:, :].unsqueeze(1).to_broadcast([P, 4, 512]), basis[q][:, :, 512 * h:512 * h + 512], ALU.mult).then_inc(S["z_done"], 1)
                        dve.wait_ge(S["m_done"], 4 * t + 2 * q + 4)
                        nc.vector.tensor_tensor(msg[q][:, :, 0:D], ps_m[q][:, :, :], T["iib1"][:, :].unsqueeze(1).to_broadcast([P, ET, D]), ALU.add).then_inc(S[f"m_bias{q}"], 1)
                        dve.wait_ge(S["summed"], g + 1)
                        place_to(*following)
                        add(g)
                dve.wait_ge(S["summed"], EGROUPS + 1)
                add(EGROUPS)

            def general(dve):
                ch = Chain(dve, V["dve"])
                nc.vector.memset(aggT[:, :], 0.0)
                ch(nc.vector.memset(msg[0][:, :, :], 1.0))
                with dve.Fori(0, EGROUPS) as g:
                    for h in range(2):
                        dve.wait_ge(V["basis"], 32 * g + 32)
                        dve.wait_ge(V["u_out"], 2 * g + h + 1)
                        dve.wait_ge(V["m"], 2 * g)
                        nc.vector.tensor_tensor(z[h][:, :, :], u[h][:, :].unsqueeze(1).to_broadcast([P, 4, 512]), basis[0][:, :, 512 * h:512 * h + 512], ALU.mult).then_inc(V["z"], 1)
                    dve.wait_ge(V["m"], 2 * g + 2)
                    dve.wait_ge(V["stored"], 16 * g)
                    nc.vector.tensor_tensor(msg[0][:, :, 0:D], ps_m[0][:, :, :], T["iib1"][:, :].unsqueeze(1).to_broadcast([P, ET, D]), ALU.add).then_inc(V["bias"], 1)
                for k in range(GT):
                    last = nc.vector.tensor_scalar(places[:, k * P:(k + 1) * P], T["iota_w"][:, :], float(k * P), None, ALU.add)
                ch(last)
                with dve.Fori(0, GROUPS) as group:
                    with dve.Fori(0, EGROUPS) as g:
                        n = group * EGROUPS + g
                        dve.wait_ge(V["back"], 32 * n + 32)
                        dve.wait_ge(V["used"], ET * n)
                        nc.vector.tensor_scalar(place[:, :], target[:, :], T["group_base"][:, bass.ds(group, 1)], None, ALU.subtract).then_inc(V["placed"], 1)
                        dve.wait_ge(V["placed"], n + 1)
                        for i in range(ET):
                            if i >= 2:
                                dve.wait_ge(V["used"], ET * n + i - 1)
                            nc.vector.tensor_scalar(hot[i % 2], places[:, :], place[:, i:i + 1], None, ALU.is_equal).then_inc(V["hot"], 1)
                    for b in range(BANKS):
                        dve.wait_ge(V["used"], ET * EGROUPS * (group + 1))
                        nc.vector.tensor_copy(aggT[:, bass.ds(group * GC + b * BC, BC)], banks[b][0:D + 1, 0:BC]).then_inc(V["taken"], 1)

            choose(dve, regular, general)

        @blk.tensor
        def _(pe):
            mm = nc.tensor.matmul

            def regular(pe):
                pe.wait_ge(S["init"], 1)
                pe.sem_inc(S["m_done"], 2)

                def sum_group(q, n, before):
                    pe.wait_ge(S[f"tanh{q}"], n)
                    pe.wait_ge(S[f"to{q}"], n)
                    pe.wait_ge(S["added"], before)
                    pe.sem_inc(S["passed"], 1)
                    for i in range(ET):
                        last = mm(ps_w[0:D + 1, :], msg[q][:, i, :], to_node[q][:, i, :], start=(i == 0), stop=(i == ET - 1))
                    last.then_inc(S["summed"], 1)

                def join(t, q):
                    pe.wait_ge(S[f"loaded{q}"], 64 * t + 64)
                    pe.wait_ge(S[f"from{q}"], t + 1)
                    pe.wait_ge(S[f"rows{q}"], 16 * ET * (t + 1))
                    for h in range(2):
                        pe.wait_ge(S["u_out"], 4 * t + 2 * q + h + 1)
                        pe.sem_inc(S["passed"], 1)
                        mm(ps_u[h][:, :], window[q][:, :], from_node[q][:, 512 * h:512 * h + 512], start=True, stop=False)
                        for i in range(4):
                            last = mm(ps_u[h][:, i * P:(i + 1) * P], gathered[q][:, 4 * h + i, :], T["ident"][:, :], start=False, stop=(i == 3))
                        last.then_inc(S[f"u{q}"], 1)

                join(0, 0)
                with pe.Fori(0, STEPS) as t:
                    for q in range(2):
                        g = 2 * t + q
                        join(*((t, 1) if q == 0 else (t + 1, 0)))
                        pe.wait_ge(S[f"m_bias{q}"], t)
                        for h in range(2):
                            pe.wait_ge(S["z_done"], 4 * t + 2 * q + h + 3)
                            pe.sem_inc(S["passed"], 1)
                            for i in range(4):
                                for k in range(4):
                                    last = mm(ps_m[q][:, 4 * h + i, :], z[h][:, k, i * P:(i + 1) * P], T["M"][:, k, :], start=(k == 0), stop=(k == 3))
                            last.then_inc(S["m_done"], 1)
                        sum_group(1 - q, t + q, g)
                sum_group(1, STEPS, EGROUPS)

            def general(pe):
                pe.wait_ge(V["dve"], 1)
                with pe.Fori(0, EGROUPS) as g:
                    pe.wait_ge(V["rows"], 32 * ET * (g + 1))
                    for h in range(2):
                        pe.wait_ge(V["u_out"], 2 * g)
                        pe.sem_inc(S["passed"], 1)
                        for i in range(4):
                            mm(ps_u[h][:, i * P:(i + 1) * P], gathered[0][:, 4 * h + i, :], T["ident"][:, :], start=True, stop=False)
                            last = mm(ps_u[h][:, i * P:(i + 1) * P], gathered[1][:, 4 * h + i, :], T["ident"][:, :], start=False, stop=True)
                        last.then_inc(V["u"], 1)
                    for h in range(2):
                        pe.wait_ge(V["z"], 2 * g + h + 1)
                        pe.wait_ge(V["bias"], g)
                        pe.sem_inc(S["passed"], 1)
                        for i in range(4):
                            for k in range(4):
                                last = mm(ps_m[0][:, 4 * h + i, :], z[h][:, k, i * P:(i + 1) * P], T["M"][:, k, :], start=(k == 0), stop=(k == 3))
                        last.then_inc(V["m"], 1)
                pe.wait_ge(V["bias"], EGROUPS)

                def add_up(n, first=False, final=False):
                    pe.wait_ge(V["back"], 32 * n + 32)
                    for i in range(ET):
                        pe.wait_ge(V["hot"], ET * n + i + 1)
                        pe.sem_inc(S["passed"], 1)
                        for b in range(BANKS):
                            last = mm(banks[b][0:D + 1, 0:BC], msg[0][:, i, :], hot[i % 2][:, BC * b:BC * b + BC], start=first and i == 0, stop=final and i == ET - 1)
                        last.then_inc(V["used"], 1)

                with pe.Fori(0, GROUPS) as group:
                    pe.wait_ge(V["taken"], BANKS * group)
                    add_up(group * EGROUPS, first=True)
                    with pe.Fori(1, EGROUPS - 1) as g:
                        add_up(group * EGROUPS + g)
                    add_up(group * EGROUPS + EGROUPS - 1, final=True)

            choose(pe, regular, general)


def after_edges(nc, T, w):
    with ExitStack() as c:
        sb = lambda n, s, d: c.enter_context(nc.sbuf_tensor(n, s, d))
        sem = lambda n: c.enter_context(nc.semaphore(n))
        W2e = sb("W2e", [D + 1, D + 1], F32)
        ps_x = c.enter_context(nc.psum_tensor("ps_x", [P, 2, 512], F32))
        half = GT // 2
        x_sb, deg = T["x"], T["deg"]
        S = {n: sem("f_" + n) for n in "w0 w used read passed".split()}
        blk = c.enter_context(nc.Block())

        @blk.sync
        def _(sp):
            sp.wait_ge(S["w0"], 2)
            sp.dma_start(W2e[0:D, 0:D], w["ii_W2"]).then_inc(S["w"], 16)
            sp.dma_start(W2e[D:D + 1, 0:D], w["ii_b2"]).then_inc(S["w"], 16)

        @blk.vector
        def _(dve):
            nc.vector.memset(W2e[:, :], 0.0).then_inc(S["w0"], 1)
            dve.wait_ge(S["w0"], 1)
            nc.vector.memset(W2e[D:D + 1, D:D + 1], 1.0).then_inc(S["w0"], 1)
            with dve.Fori(0, GROUPS) as g:
                for b in range(2):
                    dve.wait_ge(S["used"], 2 * g + b + 1)
                    got = ps_x[:, b, 0:half * (D + 1)].rearrange("p (k d) -> p k d", k=half)
                    at = bass.ds(g * GT + b * half, half)
                    nc.vector.tensor_tensor(x_sb[:, at, :], x_sb[:, at, :], got[:, :, 0:D], ALU.add)
                    nc.vector.tensor_copy(deg[:, at], got[:, :, D]).then_inc(S["read"], 1)

        @blk.tensor
        def _(pe):
            pe.wait_ge(S["w"], 32)
            for b in range(2 * GROUPS):
                if b >= 2:
                    pe.wait_ge(S["read"], b - 1)
                for i in range(half):
                    at = (b * half + i) * P
                    last = nc.tensor.matmul(ps_x[:, b % 2, i * (D + 1):(i + 1) * (D + 1)], T["aggT"][:, at:at + P], W2e[:, :], start=True, stop=True)
                last.then_inc(S["used"], 1)


GCN, LIGHT, GIN = "gcn", "light", "gin"
KINDS = [GCN, GCN, GCN, LIGHT, LIGHT, LIGHT, GIN]
TRANSPOSING = [n for n, k in enumerate(KINDS) if k != LIGHT]
NORMS = [2, 5]


def dense(nc, T, A_blocks, w, out, G):
    with ExitStack() as c:
        sb = lambda n, s, d: c.enter_context(nc.sbuf_tensor(n, s, d))
        sem = lambda n: c.enter_context(nc.semaphore(n))
        x_sb, ident, deg = T["x"], T["ident"], T["deg"]
        h = sb("h", [P, TILES, D], F32)
        table = [sb(f"table{i}", [P, TILES, 2 * D], F16) for i in range(2)]
        ring = [sb(f"ring{i}", [P, KC, GC], U8) for i in range(SLOTS)]
        agg = sb("agg", [P, GC], F32)
        hst = sb("hst", [P, GT, D], F32)
        hT = sb("hT", [P, GC], F32)
        rT = sb("rT", [D + 1, GC], F32)
        xc, sq, tmp, hb = (sb(n, [P, GT, D], F32) for n in ("xc", "sq", "tmp", "hb"))
        small = sb("small", [P, 4, GT], F32)
        inv1, inv2, t98 = (sb(n, [P, TILES], F32) for n in ("inv1", "inv2", "t98"))
        WHL = [sb(f"WHL{i}", [P, D], F32) for i in range(3)]
        WT = [sb(f"WT{i}", [P, D], F32) for i in range(3)]
        IHL, G1HL, G1T = (sb(n, [P, D], F32) for n in ("IHL", "G1HL", "G1T"))
        g1b, eps1 = sb("g1b", [D, 1], F32), sb("eps1", [P, 1], F32)
        G2 = sb("G2", [D + 1, D], F32)
        ps_a = c.enter_context(nc.psum_tensor("ps_a", [P, BANKS, 512], F32))
        ps_t = c.enter_context(nc.psum_tensor("ps_t", [P, 4, 512], F32))
        S = {n: sem("d_" + n) for n in "w w0 wready deg1 deg2 dve var root input a_free staged tp tp_out sums agg_out post read hidden hidden_out passed".split()}
        a_in = [sem(f"d_a_in{i}") for i in range(SLOTS)]
        ends = sb("ends_d", [P, 2, SLOTS], I32)
        place = sb("place_d", [P, SLOTS], F32)
        places = sb("places_d", [P, GC], F16)
        rows = sb("rows_d", [P, SLOTS, D], F32)
        hot = [t[:, :, :].rearrange("p k c -> p (k c)").bitcast(F16) for t in ring]
        V = {n: sem("g_" + n) for n in "table ends rows known gathered placed hot used".split()}
        GSTEPS = ETILES // SLOTS
        assert GSTEPS * SLOTS == ETILES
        half = GT // 2
        cols = [512, 512, 512, GC - 3 * 512]
        wide = [P, GT, D]
        blk = c.enter_context(nc.Block())

        @blk.sync
        def _(sp):
            sp.wait_ge(S["w0"], 1)
            for i, n in enumerate(("gcn_W1T", "gcn_W2T", "gcn_W3T")):
                for t, p0 in ((WHL[i], 0), (WHL[i], D), (WT[i], 0)):
                    sp.dma_start(t[p0:p0 + D, :], w[n]).then_inc(S["w"], 16)
            for t, p0 in ((G1HL, 0), (G1HL, D), (G1T, 0)):
                sp.dma_start(t[p0:p0 + D, :], w["gin_W1T"]).then_inc(S["w"], 16)
            sp.dma_start(g1b[:, :], w["gin_b1"]).then_inc(S["w"], 16)
            sp.dma_start(eps1[:, :], w["gin_eps"].to_broadcast([P, 1])).then_inc(S["w"], 16)
            sp.dma_start(G2[0:D, :], w["gin_W2T"]).then_inc(S["w"], 16)
            sp.dma_start(G2[D:D + 1, :], w["gin_b2"]).then_inc(S["w"], 16)
            flag = sp.value_load(G["irregular"], min_val=0, max_val=1)

            with sp.If(flag < 1):
                for n in range(LAYERS):
                    with sp.Fori(0, GROUPS) as g:
                        for k in range(CHUNKS):
                            sp.wait_ge(S["a_free"], (GROUPS * n + g) * CHUNKS + (k + 1))
                            sp.sem_inc(S["passed"], 1)
                            block = A_blocks[bass.ds(g, 1), :, KC * k:KC * k + KC, :].rearrange("g p k c -> p (g k) c")
                            sp.dma_start(ring[k % SLOTS][:, :, :], block).then_inc(a_in[k % SLOTS], 16)
            with sp.Else():
                for n in range(LAYERS):
                    sp.wait_ge(S["input"], GROUPS * (n + 1))
                    sp.sem_inc(S["passed"], 1)
                    sp.dma_start(G["rows"].rearrange("(k p) d -> p k d", p=P), table[n % 2][:, :, :].bitcast(F32)).then_inc(V["table"], 16)
            sp.wait_ge(S["input"], GROUPS * (LAYERS + 1))
            sp.dma_start(out[0:(TILES - 1) * P, :].rearrange("(k p) d -> p k d", p=P), x_sb[:, 0:TILES - 1, :]).then_inc(S["w"], 16)
            sp.dma_start(out[(TILES - 1) * P:N_NODES, :], x_sb[0:TAIL, TILES - 1, :]).then_inc(S["w"], 16)
            sp.wait_ge(S["w"], 16 * 18)

        @blk.gpsimd
        def _(pool):
            flag = pool.value_load(G["irregular"], min_val=0, max_val=1)

            def gather_edges(n, g):
                pool.wait_ge(V["table"], 16 * (n + 1))
                with pool.Fori(0, GSTEPS) as e:
                    pool.wait_ge(V["used"], (GROUPS * n + g) * GSTEPS + e)
                    pool.sem_inc(S["passed"], 1)
                    pool.dma_start(ends[:, 0, :], G["src"][:, bass.ds(e * SLOTS, SLOTS)]).then_inc(V["ends"], 16)
                    pool.dma_start(ends[:, 1, :], G["dst"][:, bass.ds(e * SLOTS, SLOTS)]).then_inc(V["ends"], 16)
                    pool.wait_ge(V["ends"], 32 * e + 32)
                    pool.sem_inc(V["known"], 1)
                    for i in range(SLOTS):
                        pool.indirect_dma_start(rows[:, i, :], None, G["rows"], bass.IndirectOffsetOnAxis(ap=ends[:, 0, i:i + 1], axis=0)).then_inc(V["rows"], 16)
                    pool.wait_ge(V["rows"], 16 * SLOTS * e + 16 * SLOTS)
                    pool.sem_inc(V["gathered"], 1)
                pool.sem_inc(S["passed"], 1)
                pool.dma_reset()
                pool.sem_clear(V["rows"])
                pool.sem_clear(V["ends"])

            for n in range(LAYERS):
                with pool.Fori(0, GROUPS) as g:
                    if n in TRANSPOSING:
                        pool.wait_ge(S["input"], GROUPS * n + g + 1)
                        j = TRANSPOSING.index(n)
                        pool.wait_ge(S["tp"], 4 * (GROUPS * j + g))
                        nc.gpsimd.tensor_copy(hst[:, :, :], h[:, bass.ds(g * GT, GT), :]).then_inc(S["staged"], 1)
                    with pool.If(flag > 0):
                        gather_edges(n, g)
                    pool.sem_inc(S["passed"], 1)

        @blk.scalar
        def _(act):
            act.wait_ge(S["deg1"], 2)
            nc.scalar.activation(inv1[:, :], inv1[:, :], ACT.Sqrt).then_inc(S["deg2"], 1)
            nc.scalar.activation(inv2[:, :], inv2[:, :], ACT.Sqrt).then_inc(S["deg2"], 1)

            def root(n):
                act.wait_ge(S["var"], n)
                nc.scalar.activation(small[:, 2, :], small[:, 2, :], ACT.Sqrt, bias=T["eps"][:, :]).then_inc(S["root"], 1)

            with act.Fori(0, GROUPS) as g:
                root(g + 1)
            def take_sums(n, g):
                if n in TRANSPOSING:
                    j = GROUPS * TRANSPOSING.index(n) + g
                    for b in range(4):
                        act.wait_ge(S["tp"], 4 * j + (b + 1))
                        nc.scalar.copy(hT[0:D, 512 * b:512 * b + cols[b]], ps_t[0:D, b, 0:cols[b]]).then_inc(S["tp_out"], 1)
                for b in range(BANKS):
                    act.wait_ge(S["sums"], BANKS * (GROUPS * n + g) + (b + 1))
                    nc.scalar.copy(agg[:, BC * b:BC * b + BC], ps_a[:, b, 0:BC]).then_inc(S["agg_out"], 1)

            def help_output(n, g):
                if KINDS[n] == GIN:
                    for b in range(BANKS):
                        act.wait_ge(S["hidden"], 4 * g + (b + 1))
                        nc.scalar.activation(rT[0:D, BC * b:BC * b + BC], ps_t[0:D, b, 0:BC], ACT.Relu, bias=g1b[:, :]).then_inc(S["hidden_out"], 1)
                if n in NORMS:
                    root(GROUPS * (1 + NORMS.index(n)) + g + 1)

            for n in range(LAYERS):
                if n:
                    help_output(n - 1, GROUPS - 1)
                take_sums(n, 0)
                with act.Fori(1, GROUPS) as g:
                    help_output(n, g - 1)
                    take_sums(n, g)
            help_output(LAYERS - 1, GROUPS - 1)

        @blk.vector
        def _(dve):
            ch = Chain(dve, S["dve"])
            for t in (*WT, G1T):
                nc.vector.memset(t[D:P, :], 0.0)
            nc.vector.memset(hT[D:P, :], 0.0)
            nc.vector.memset(rT[D:D + 1, :], 1.0)
            nc.vector.tensor_copy(IHL[0:D, :], ident[0:D, 0:D])
            nc.vector.tensor_scalar(IHL[D:P, :], ident[D:P, D:P], 1.0 / LO, None, ALU.mult).then_inc(S["w0"], 1)
            nc.vector.tensor_scalar(inv1[:, :], deg[:, :], 1.0, None, ALU.add).then_inc(S["deg1"], 1)
            nc.vector.tensor_scalar(inv2[:, :], deg[:, :], 1.0, None, ALU.max).then_inc(S["deg1"], 1)
            ch(nc.vector.tensor_scalar(t98[:, :], deg[:, :], 0.0, None, ALU.is_gt))
            dve.wait_ge(S["deg2"], 2)
            nc.vector.reciprocal(inv1[:, :], inv1[:, :])
            ch(nc.vector.reciprocal(inv2[:, :], inv2[:, :]))
            ch(nc.vector.tensor_tensor(inv2[:, :], inv2[:, :], t98[:, :], ALU.mult))
            dve.wait_ge(S["w"], 16 * 16)
            for t in (*WHL, G1HL):
                nc.vector.tensor_scalar(t[D:P, :], t[D:P, :], 1.0 / LO, None, ALU.mult)
            ch(nc.vector.tensor_scalar(eps1[:, :], eps1[:, :], 1.0, None, ALU.add))
            nc.vector.tensor_scalar(G1T[0:D, :], G1T[0:D, :], eps1[0:D, :], None, ALU.mult).then_inc(S["wready"], 1)

            def scaled(ch, v, inv, g):
                ch(nc.vector.tensor_tensor(tmp[:, :, :], v, inv[:, bass.ds(g * GT, GT)].unsqueeze(2).to_broadcast(wide), ALU.mult))
                return tmp[:, :, :]

            def norm(ch, at, to, n):
                dve.sem_inc(S["passed"], 1)
                ch(centre_and_scale(nc, ch, x_sb[:, at, :], xc[:, :, :], sq[:, :, :], small, to, S["var"], S["root"], n))

            for k in range(GT):
                nc.vector.tensor_scalar(places[:, k * P:(k + 1) * P], T["iota_w"][:, :], float(k * P), None, ALU.add).then_inc(V["placed"], 1)
            flag = dve.value_load(G["irregular"], min_val=0, max_val=1)

            def place_edges(n, g):
                with dve.Fori(0, GSTEPS) as e:
                    m = (GROUPS * n + g) * GSTEPS + e
                    dve.wait_ge(V["known"], m + 1)
                    dve.wait_ge(V["used"], m)
                    nc.vector.tensor_scalar(place[:, :], ends[:, 1, :], T["group_base"][:, bass.ds(g, 1)], None, ALU.subtract).then_inc(V["placed"], 1)
                    dve.wait_ge(V["placed"], GT + m + 1)
                    for i in range(SLOTS):
                        nc.vector.tensor_scalar(hot[i], places[:, :], place[:, i:i + 1], None, ALU.is_equal).then_inc(V["hot"], 1)

            def loop(start, body):
                with dve.Fori(0, GROUPS) as g:
                    step = STEPS_OF[body.__name__]
                    if loops[0]:
                        with dve.If(flag > 0):
                            place_edges(loops[0] - 1, g)
                        dve.sem_inc(S["passed"], 1)
                    ch = Chain(dve, S["dve"], start + g * step)
                    body(ch, g, bass.ds(g * GT, GT))
                    dve.wait_ge(S["input"], GROUPS * loops[0] + g + 1)
                    assert ch.n == step, (body.__name__, ch.n)
                loops[0] += 1
                return start + GROUPS * step

            loops = [0]
            STEPS_OF = {"first": 9, "gcn": 4, "gcn_last": 11, "light": 4, "light_last": 9, "gin": 0}

            def first(ch, g, at):
                norm(ch, at, h[:, at, :], g + 1)
                split(nc, ch, scaled(ch, h[:, at, :], inv1, g), table[0][:, at, :], sq[:, :, :]).then_inc(S["input"], 1)

            start = loop(ch.n, first)
            for n, kind in enumerate(KINDS):
                to = table[(n + 1) % 2]

                def got(g, b):
                    dve.wait_ge(S["post"], 2 * (GROUPS * n + g) + (b + 1))
                    return ps_t[:, b, 0:half * D].rearrange("p (k d) -> p k d", k=half)

                def factor(inv, g, b):
                    return inv[:, bass.ds(g * GT + b * half, half)].unsqueeze(2).to_broadcast([P, half, D])

                def gcn(ch, g, at):
                    for b in range(2):
                        last = nc.vector.scalar_tensor_tensor(out=hb[:, b * half:(b + 1) * half, :], in0=got(g, b), scalar=0.0, in1=factor(inv1, g, b), op0=ALU.max, op1=ALU.mult)
                    last.then_inc(S["read"], 1)
                    dve.wait_ge(S["read"], GROUPS * n + g + 1)
                    ch(nc.vector.tensor_copy(h[:, at, :], hb[:, :, :]))
                    split(nc, ch, scaled(ch, hb[:, :, :], inv1, g), to[:, at, :], sq[:, :, :]).then_inc(S["input"], 1)

                def gcn_last(ch, g, at):
                    for b in range(2):
                        last = nc.vector.scalar_tensor_tensor(out=hb[:, b * half:(b + 1) * half, :], in0=got(g, b), scalar=0.0, in1=factor(inv1, g, b), op0=ALU.max, op1=ALU.mult)
                    last.then_inc(S["read"], 1)
                    dve.wait_ge(S["read"], GROUPS * n + g + 1)
                    ch(nc.vector.tensor_tensor(x_sb[:, at, :], x_sb[:, at, :], hb[:, :, :], ALU.add))
                    norm(ch, at, hb[:, :, :], GROUPS + g + 1)
                    ch(nc.vector.scalar_tensor_tensor(out=x_sb[:, at, :], in0=hb[:, :, :], scalar=0.25, in1=x_sb[:, at, :], op0=ALU.mult, op1=ALU.add))
                    split(nc, ch, scaled(ch, hb[:, :, :], inv2, g), to[:, at, :], sq[:, :, :]).then_inc(S["input"], 1)

                def light_sum(ch, g, at):
                    for b in range(2):
                        last = nc.vector.tensor_tensor(hb[:, b * half:(b + 1) * half, :], got(g, b), factor(inv2, g, b), ALU.mult)
                    last.then_inc(S["read"], 1)
                    dve.wait_ge(S["read"], GROUPS * n + g + 1)
                    ch(nc.vector.scalar_tensor_tensor(out=x_sb[:, at, :], in0=hb[:, :, :], scalar=0.25, in1=x_sb[:, at, :], op0=ALU.mult, op1=ALU.add))

                def light(ch, g, at):
                    light_sum(ch, g, at)
                    split(nc, ch, scaled(ch, hb[:, :, :], inv2, g), to[:, at, :], sq[:, :, :]).then_inc(S["input"], 1)

                def light_last(ch, g, at):
                    light_sum(ch, g, at)
                    norm(ch, at, h[:, at, :], 2 * GROUPS + g + 1)
                    split(nc, ch, h[:, at, :], to[:, at, :], sq[:, :, :]).then_inc(S["input"], 1)

                def gin(ch, g, at):
                    for b in range(2):
                        half_at = bass.ds(g * GT + b * half, half)
                        last = nc.vector.tensor_tensor(x_sb[:, half_at, :], got(g, b), x_sb[:, half_at, :], ALU.add)
                        if b:
                            last.then_inc(S["input"], 1)
                        else:
                            last.then_inc(S["read"], 1)

                body = {GCN: gcn_last if n in NORMS else gcn, LIGHT: light_last if n in NORMS else light, GIN: gin}[kind]
                start = loop(start, body)

        @blk.tensor
        def _(pe):
            mm = nc.tensor.matmul
            pe.sem_inc(S["a_free"], SLOTS)
            flag = pe.value_load(G["irregular"], min_val=0, max_val=1)

            def add_edges(G_, e, first=False, final=False):
                m = G_ * GSTEPS + e
                pe.wait_ge(V["gathered"], m + 1)
                pe.wait_ge(V["hot"], SLOTS * (m + 1))
                pe.sem_inc(S["passed"], 1)
                for i in range(SLOTS):
                    for b in range(BANKS):
                        last = mm(ps_a[:, b, 0:BC], rows[:, i, :].bitcast(F16), hot[i][:, BC * b:BC * b + BC], start=first and i == 0, stop=final and i == SLOTS - 1)
                last.then_inc(V["used"], 1)

            def blocks(n, G_, segment, first):
                for k in range(segment * SLOTS, (segment + 1) * SLOTS):
                    pe.wait_ge(a_in[k % SLOTS], 16 * (CHUNKS // SLOTS * G_ + (segment + 1)))
                    if first:
                        pe.wait_ge(S["input"], GROUPS * n + (KC * k + KC - 1) // GT + 1)
                    pe.sem_inc(S["passed"], 1)
                    by_bank = k in (0, CHUNKS - 1)
                    order = [(i, b) for b in range(BANKS) for i in range(KC)] if by_bank else [(i, b) for i in range(KC) for b in range(BANKS)]
                    for i, b in order:
                        if k == 0 and i == 0 and not (first and n == 0):
                            pe.wait_ge(S["agg_out"], BANKS * G_ + (b + 1 - BANKS))
                            pe.sem_inc(S["a_free"] if b == BANKS - 1 else S["passed"], 1)
                        last_tile = k == CHUNKS - 1 and i == KC - 1
                        last = mm(ps_a[:, b, 0:BC], table[n % 2][:, KC * k + i, :], ring[k % SLOTS][:, i, BC * b:BC * b + BC].bitcast(F8), start=(k == 0 and i == 0), stop=last_tile)
                        if last_tile:
                            last.then_inc(S["sums"], 1)
                    if k < CHUNKS - 1:
                        last.then_inc(S["a_free"], 1)

            def transpose_input(n, g):
                pe.wait_ge(S["staged"], GROUPS * TRANSPOSING.index(n) + g + 1)
                if n == LAYERS - 1:
                    pe.wait_ge(S["input"], GROUPS * (n + 1) + g)
                else:
                    pe.wait_ge(S["read"], GROUPS * n + g)
                pe.sem_inc(S["passed"], 1)
                for t in range(GT):
                    last = nc.tensor.transpose(ps_t[0:D, t // 4, (t % 4) * P:(t % 4 + 1) * P], hst[:, t, :], ident[:, :])
                    if t % 4 == 3 or t == GT - 1:
                        last.then_inc(S["tp"], 1)

            def begin_output(n, g):
                if n in TRANSPOSING:
                    pe.wait_ge(S["tp_out"], 4 * (GROUPS * TRANSPOSING.index(n) + g) + 4)
                else:
                    pe.wait_ge(S["read"], GROUPS * n + g)
                pe.wait_ge(S["agg_out"], BANKS * (GROUPS * n + g) + BANKS)
                pe.sem_inc(S["passed"], 1)
                if KINDS[n] == GIN:
                    for b in range(BANKS):
                        at = slice(BC * b, BC * b + BC)
                        mm(ps_t[0:D, b, 0:BC], G1HL[:, :], agg[:, at], start=True, stop=False)
                        mm(ps_t[0:D, b, 0:BC], G1T[:, :], hT[:, at], start=False, stop=True).then_inc(S["hidden"], 1)
                else:
                    output(n)

            def end_output(n, g):
                if KINDS[n] == GIN:
                    pe.wait_ge(S["hidden_out"], 4 * g + 4)
                    pe.sem_inc(S["passed"], 1)
                    output(n)

            def output(n):
                for t in range(GT):
                    o = ps_t[:, t // half, (t % half) * D:(t % half + 1) * D]
                    at = slice(t * P, (t + 1) * P)
                    if KINDS[n] == GCN:
                        mm(o, agg[:, at], WHL[n][:, :], start=True, stop=False)
                        last = mm(o, hT[:, at], WT[n][:, :], start=False, stop=True)
                    elif KINDS[n] == LIGHT:
                        last = mm(o, agg[:, at], IHL[:, :], start=True, stop=True)
                    else:
                        last = mm(o, rT[:, at], G2[:, :], start=True, stop=True)
                    if t % half == half - 1:
                        last.then_inc(S["post"], 1)

            def group(n, g, before, first=False):
                G_ = GROUPS * n + g
                with pe.If(flag < 1):
                    blocks(n, G_, 0, first)
                if before:
                    begin_output(*before)
                with pe.If(flag < 1):
                    blocks(n, G_, 1, first)
                if before:
                    end_output(*before)
                with pe.If(flag < 1):
                    blocks(n, G_, 2, first)
                if n in TRANSPOSING:
                    transpose_input(n, g)
                with pe.If(flag < 1):
                    for segment in range(3, CHUNKS // SLOTS):
                        blocks(n, G_, segment, first)
                with pe.Else():
                    pe.wait_ge(S["agg_out"], BANKS * G_)
                    add_edges(G_, 0, first=True)
                    with pe.Fori(1, GSTEPS - 1) as e:
                        add_edges(G_, e)
                    add_edges(G_, GSTEPS - 1, final=True)
                    pe.wait_ge(V["used"], G_ * GSTEPS + GSTEPS)
                    pe.sem_inc(S["sums"], BANKS)

            pe.wait_ge(S["wready"], 1)
            for n in range(LAYERS):
                group(n, 0, (n - 1, GROUPS - 1) if n else None, first=True)
                with pe.Fori(1, GROUPS) as g:
                    group(n, g, (n, g - 1))
                    pe.sem_inc(S["passed"], 1)
            begin_output(LAYERS - 1, GROUPS - 1)
            end_output(LAYERS - 1, GROUPS - 1)


def padded_edges(src, dst):
    after = P * SPAN + SHIFTS - N_EDGES
    i = np.arange(after, dtype=np.int32)
    lead = np.full(SHIFTS, NP - 1, np.int32)
    return (np.concatenate([lead, src, NP - 1 - i % 3]).astype(np.int32),
            np.concatenate([lead, dst, N_NODES + i // 3]).astype(np.int32))


def lay_out(x, src, dst, edge_attr_8, **w):
    flat = np.ascontiguousarray
    pad = EP - N_EDGES
    src_row, dst_row = padded_edges(src, dst)
    tiles = lambda a, v: flat(np.concatenate([a, np.full(pad, v, np.int32)]).reshape(ETILES, P).T)
    return {
        "x": x, "src_row": src_row, "dst_row": dst_row,
        "srcT": tiles(src, 0), "dstT": tiles(dst, NP - 1),
        "dst_seq": np.concatenate([np.zeros(EG, np.int32), dst, np.full(pad + EG, NP - 1, np.int32)]),
        "basisT": flat(np.concatenate([edge_attr_8, np.zeros((pad + EG, NB), np.float32)]).T),
        "pp_W1": w["L0_gnn_pp_W1"], "pp_b1": w["L0_gnn_pp_b1"].reshape(D, 1),
        "pp_W2": w["L0_gnn_pp_W2"], "pp_b2": w["L0_gnn_pp_b2"].reshape(D, 1),
        "pi_W1T": flat(w["L0_gnn_pi_W1"].reshape(2, D, D).transpose(2, 0, 1)).reshape(D, 2 * D),
        "pi_b1": w["L0_gnn_pi_b1"].reshape(D, 1), "pi_W2": w["L0_gnn_pi_W2"], "pi_b2": w["L0_gnn_pi_b2"].reshape(D, 1),
        "pi_W3T": flat(w["L0_gnn_pi_W3"].reshape(D, D, NB).transpose(1, 2, 0)),
        "ii_W1": w["L0_gnn_ii_W1"], "ii_b1": w["L0_gnn_ii_b1"].reshape(1, D),
        "ii_W2": w["L0_gnn_ii_W2"], "ii_b2": w["L0_gnn_ii_b2"].reshape(1, D),
        "gcn_W1T": flat(w["L1_gnn_W1"].T), "gcn_W2T": flat(w["L1_gnn_W2"].T), "gcn_W3T": flat(w["L1_gnn_W3"].T),
        "gin_eps": w["L3_gnn_eps"].reshape(1, 1), "gin_W1T": flat(w["L3_gnn_W1"].T), "gin_b1": w["L3_gnn_b1"].reshape(D, 1),
        "gin_W2T": flat(w["L3_gnn_W2"].T), "gin_b2": w["L3_gnn_b2"].reshape(1, D),
    }


def kernel(**inputs):
    import concourse.bacc as bacc
    from concourse.bass_utils import run_bass_kernel_spmd

    nc = bacc.Bacc("TRN2", target_bir_lowering=False, num_devices=1)
    arrays = lay_out(**{k: np.asarray(v) for k, v in inputs.items()})
    aps = {k: nc.dram_tensor("in_" + k, a.shape, mybir.dt.from_np(a.dtype), kind="ExternalInput").ap() for k, a in arrays.items()}
    out = nc.dram_tensor("out", (N_NODES, D), F32, kind="ExternalOutput").ap()
    build(nc, aps, out)
    r = run_bass_kernel_spmd(nc, [{"in_" + k: a for k, a in arrays.items()}], core_ids=[0])
    return r.results[0]["out"]
```
